# Optimizing a Trainium2 kernel written in Bass

```python
import numpy as np
import jax
import jax.numpy as jnp

def _softmax(x, axis=-1):
    return jax.nn.softmax(x, axis=axis)

def _gelu(x):
    return jax.nn.gelu(x, approximate=True)

def _silu(x):
    return jax.nn.silu(x)

def _sigmoid(x):
    return jax.nn.sigmoid(x)

def _layernorm(x, axis=-1, eps=1e-05):
    m = jnp.mean(x, axis=axis, keepdims=True)
    v = jnp.var(x, axis=axis, keepdims=True)
    return (x - m) / jnp.sqrt(v + eps)

def _scatter_add(tgt, idx, src, axis=0):
    return tgt.at[idx].add(src)

def _segment_sum(src, seg, n):
    return jax.ops.segment_sum(src, seg, n)
kernel_name = 'mk_xattn_seq_d1_seqx_r8_836d87'

def setup_inputs(seed: int=0):
    np.random.seed(seed)
    _w = jnp.asarray

    def _rec_inputs():
        import jax
        import jax.numpy as jnp
        _rk = jax.random.key(seed)
        x = -0.0002928 + 1 * jax.random.normal(jax.random.fold_in(_rk, 1), (128, 64, 128), jnp.float32)
        _lenS = 64 - jax.random.randint(jax.random.fold_in(_rk, 7), (128,), 0, max(1, 64 // 4) + 1, jnp.int32)
        _lenS2 = 64 - jax.random.randint(jax.random.fold_in(_rk, 8), (128,), 0, max(1, 64 // 4) + 1, jnp.int32)
        _ctx_1024P = jax.random.normal(jax.random.fold_in(_rk, 11), (128, 16, 128), jnp.float32)
        _ctx_1024c = jax.random.dirichlet(jax.random.fold_in(_rk, 511), 0.3 * jnp.ones((16,), jnp.float32), (128, 64))
        _ctx_1024t = jnp.einsum('bsk,bkd->bsd', _ctx_1024c, _ctx_1024P)
        _ctx_1024t = _ctx_1024t * jax.lax.rsqrt(jnp.mean(jnp.square(_ctx_1024t)) + 1e-12) * 0.953939
        ctx_1024 = 4.13588e-05 + 0.999923 * (_ctx_1024t + 0.3 * jax.random.normal(jax.random.fold_in(_rk, 611), (128, 64, 128), jnp.float32))
        return (x, ctx_1024)
    x, ctx_1024 = _rec_inputs()

    def _L0_xattn_setup():
        import jax, jax.numpy as jnp
        import numpy as np
        DIM = 128
        HEADS = 16
        D_HEAD = 64
        INNER = HEADS * D_HEAD
        FF_INNER = 4 * DIM

        def _block(x, context, Wq, Wk, Wv, Wo, bo, W1, b1, W2, b2):
            B, Lq, _ = x.shape
            scale = 1.0 / np.sqrt(D_HEAD).astype(np.float32)
            q = (x @ Wq).reshape(B, Lq, HEADS, D_HEAD)
            k = (context @ Wk).reshape(B, -1, HEADS, D_HEAD)
            v = (context @ Wv).reshape(B, -1, HEADS, D_HEAD)
            sim = jnp.einsum('bqhd,bkhd->bhqk', q, k) * scale
            attn = jax.nn.softmax(sim, axis=-1)
            out = jnp.einsum('bhqk,bkhd->bqhd', attn, v).reshape(B, Lq, INNER)
            x = out @ Wo + bo + x
            h = jax.nn.gelu(x @ W1 + b1, approximate=False)
            return h @ W2 + b2 + x
        key = jax.random.key(seed)
        ks = jax.random.split(key, 12)
        s = lambda fan_in: 1.0 / np.sqrt(fan_in)
        x = jax.random.normal(ks[0], (4, 128, DIM), dtype=jnp.float32)
        context = jax.random.normal(ks[1], (4, 256, DIM), dtype=jnp.float32)
        Wq = jax.random.normal(ks[2], (DIM, INNER), dtype=jnp.float32) * s(DIM)
        Wk = jax.random.normal(ks[3], (DIM, INNER), dtype=jnp.float32) * s(DIM)
        Wv = jax.random.normal(ks[4], (DIM, INNER), dtype=jnp.float32) * s(DIM)
        Wo = jax.random.normal(ks[5], (INNER, DIM), dtype=jnp.float32) * s(INNER)
        bo = jax.random.normal(ks[6], (DIM,), dtype=jnp.float32) * 0.01
        W1 = jax.random.normal(ks[7], (DIM, FF_INNER), dtype=jnp.float32) * s(DIM)
        b1 = jax.random.normal(ks[8], (FF_INNER,), dtype=jnp.float32) * 0.01
        W2 = jax.random.normal(ks[9], (FF_INNER, DIM), dtype=jnp.float32) * s(FF_INNER)
        b2 = jax.random.normal(ks[10], (DIM,), dtype=jnp.float32) * 0.01
        return {'x': x, 'context': context, 'Wq': Wq, 'Wk': Wk, 'Wv': Wv, 'Wo': Wo, 'bo': bo, 'W1': W1, 'b1': b1, 'W2': W2, 'b2': b2}
    _L0_xattn_all = _L0_xattn_setup()
    _L0_xattn_in = {k: v for k, v in _L0_xattn_all.items() if k in ('Wq', 'Wk', 'Wv', 'Wo', 'bo', 'W1', 'b1', 'W2', 'b2')}
    del _L0_xattn_all
    return {'x': x, 'ctx_1024': ctx_1024, 'L0_xattn_Wq': _L0_xattn_in['Wq'], 'L0_xattn_Wk': _L0_xattn_in['Wk'], 'L0_xattn_Wv': _L0_xattn_in['Wv'], 'L0_xattn_Wo': _L0_xattn_in['Wo'], 'L0_xattn_bo': _L0_xattn_in['bo'], 'L0_xattn_W1': _L0_xattn_in['W1'], 'L0_xattn_b1': _L0_xattn_in['b1'], 'L0_xattn_W2': _L0_xattn_in['W2'], 'L0_xattn_b2': _L0_xattn_in['b2']}

def reference(x, ctx_1024, L0_xattn_Wq, L0_xattn_Wk, L0_xattn_Wv, L0_xattn_Wo, L0_xattn_bo, L0_xattn_W1, L0_xattn_b1, L0_xattn_W2, L0_xattn_b2):
    import jax
    import jax.numpy as jnp

    def _L0_xattn_ref(x, context, Wq, Wk, Wv, Wo, bo, W1, b1, W2, b2):
        import jax, jax.numpy as jnp
        import numpy as np
        DIM = 128
        HEADS = 16
        D_HEAD = 64
        INNER = HEADS * D_HEAD
        FF_INNER = 4 * DIM

        def _block(x, context, Wq, Wk, Wv, Wo, bo, W1, b1, W2, b2):
            B, Lq, _ = x.shape
            scale = 1.0 / np.sqrt(D_HEAD).astype(np.float32)
            q = (x @ Wq).reshape(B, Lq, HEADS, D_HEAD)
            k = (context @ Wk).reshape(B, -1, HEADS, D_HEAD)
            v = (context @ Wv).reshape(B, -1, HEADS, D_HEAD)
            sim = jnp.einsum('bqhd,bkhd->bhqk', q, k) * scale
            attn = jax.nn.softmax(sim, axis=-1)
            out = jnp.einsum('bhqk,bkhd->bqhd', attn, v).reshape(B, Lq, INNER)
            x = out @ Wo + bo + x
            h = jax.nn.gelu(x @ W1 + b1, approximate=False)
            return h @ W2 + b2 + x
        return _block(x, context, Wq, Wk, Wv, Wo, bo, W1, b1, W2, b2)
    x = _L0_xattn_ref(x, ctx_1024, L0_xattn_Wq, L0_xattn_Wk, L0_xattn_Wv, L0_xattn_Wo, L0_xattn_bo, L0_xattn_W1, L0_xattn_b1, L0_xattn_W2, L0_xattn_b2)
    return x

_drawn_inputs = setup_inputs


def setup_inputs(seed=0):
    import zlib

    import numpy as np

    out = dict(_drawn_inputs(seed))
    spreads = {}
    factors = {'L0_xattn_bo': 6.166, 'L0_xattn_b1': 8.0, 'L0_xattn_b2': 6.88}
    for name, (base, spread) in spreads.items():
        noise = np.random.default_rng([zlib.crc32(name.encode()), seed]).standard_normal(out[name].shape)
        drawn = base * np.exp(spread * noise) if base else spread * noise
        out[name] = jnp.asarray(drawn.astype(out[name].dtype))
    for name, factor in factors.items():
        out[name] = (out[name] * factor).astype(out[name].dtype)
    return out
```

```python
from contextlib import ExitStack

import concourse.bass as bass
from concourse import mybir

FP32 = mybir.dt.float32
FP32R = mybir.dt.float32r
ALU = mybir.AluOpType
ACT = mybir.ActivationFunctionType
AX = mybir.AxisListType


def cross_attention_block(nc, x, context, wq, wk, wv, wo, bo, w1, b1, w2, b2, out):
    sequences, length, dim = x.shape
    inner = wq.shape[1]
    ff = w1.shape[1]
    d_head = 64
    P = 128
    HP = inner // P
    FC = ff // P
    tokens = sequences * length
    PAIRS = tokens // P
    GROUPS = PAIRS // 2
    GT = 2 * P
    HALF = HP // 2
    BANK = 512
    Q = 32
    SCALE = float(d_head) ** -0.5
    ROUNDS = PAIRS // 4
    FT = 4 * P
    FSTEPS = tokens // FT

    x_rows = x.rearrange("b l d -> (b l) d").rearrange("(t p) d -> p t d", p=P)
    c_rows = context.rearrange("b l d -> (b l) d").rearrange("(t p) d -> p t d", p=P)
    out_rows = out.rearrange("b l d -> (b l) d").rearrange("(t p) d -> p t d", p=P)

    with ExitStack() as outer:
        def sb(name, shape, dt=FP32, to=outer):
            return to.enter_context(nc.sbuf_tensor(name, shape, dt))

        def sem(name, to=outer):
            return to.enter_context(nc.semaphore(name))

        bank = [outer.enter_context(nc.psum_tensor(f"bank{n}", [P, BANK], FP32)) for n in range(8)]

        ident = sb("ident", [P, P])
        wq_hi, wq_lo = sb("wq_hi", [P, inner], FP32R), sb("wq_lo", [P, inner], FP32R)
        wk_hi, wk_lo = sb("wk_hi", [P, inner], FP32R), sb("wk_lo", [P, inner], FP32R)
        vo_hi, vo_lo = sb("vo_hi", [P, 2, HP, dim], FP32R), sb("vo_lo", [P, 2, HP, dim], FP32R)
        w1_hi, w1_lo = sb("w1_hi", [P, ff], FP32R), sb("w1_lo", [P, ff], FP32R)
        w2_hi, w2_lo = sb("w2_hi", [P, FC, dim], FP32R), sb("w2_lo", [P, FC, dim], FP32R)
        bo_all = sb("bo_all", [P, dim])
        b1_col, b2_col = sb("b1_col", [P, FC]), sb("b2_col", [P, 1])
        x1 = sb("x1", [P, PAIRS, dim])

        with ExitStack() as ctx:
            xt_in = [sb(f"x_in{n}", [P, 2, dim], to=ctx) for n in range(2)]
            ct_in = [sb(f"c_in{n}", [P, 2, dim], to=ctx) for n in range(2)]
            xT_hi = [sb(f"xT_hi{n}", [P, GT], FP32R, ctx) for n in range(2)]
            xT_lo = [sb(f"xT_lo{n}", [P, GT], FP32R, ctx) for n in range(2)]
            cT_hi = [sb(f"cT_hi{n}", [P, 2, 3 * length], FP32R, ctx) for n in range(2)]
            cT_lo = [sb(f"cT_lo{n}", [P, 2, 3 * length], FP32R, ctx) for n in range(2)]
            cvo = [sb(f"cvo{n}", [P, 2, HP, dim], to=ctx) for n in range(4)]
            probs = [sb(f"probs{n}", [P, 2 * HP, length], to=ctx) for n in range(2)]
            blocksT = [sb(f"blocksT{n}", [P, 4, Q, 2, HP], to=ctx) for n in range(2)]
            probsT = [sb(f"probsT{n}", [P, 4, Q, 2, HP], to=ctx) for n in range(2)]
            wq_f, wk_f, wv_f = blocksT[0][:, 0:2], blocksT[0][:, 2:4], blocksT[1][:, 0:2]
            wo_f, wvT = blocksT[1][:, 2:4], probsT[0][:, 0:2]
            wq_f, wk_f, wv_f = (w.rearrange("p a b c d -> p (a b c d)") for w in (wq_f, wk_f, wv_f))
            wo_f, wvT = (w.rearrange("p a b c d -> p (a b c d)").rearrange("p (h n) -> p h n", h=HP)
                         for w in (wo_f, wvT))
            w1_f, w2_f = (probsT[1][:, n, :, :, :].rearrange("p b c d -> p (b c d)") for n in range(2))
            w2_f = w2_f.rearrange("p (c n) -> p c n", c=FC)
            top = [sb(f"top{n}", [P, 2 * HP], to=ctx) for n in range(2)]
            total = [sb(f"total{n}", [P, 2 * HP], to=ctx) for n in range(2)]
            inverse = [sb(f"inverse{n}", [P, 2 * HP], to=ctx) for n in range(2)]

            score_bank, proj_bank, turn_bank, out_bank = bank[0:2], bank[2:6], bank[6], bank[7]
            vo_bank = [bank[0], bank[1], bank[7], bank[6]]

            wq_loaded, wk_loaded = sem("wq_loaded", ctx), sem("wk_loaded", ctx)
            wv_loaded, wo_loaded = sem("wv_loaded", ctx), sem("wo_loaded", ctx)
            w12_loaded, w12_hi = sem("w12_loaded", ctx), sem("w12_hi", ctx)
            w12_ready = sem("w12_ready", ctx)
            biases_loaded = sem("biases_loaded", ctx)
            zeroed, ident_ready = sem("zeroed", ctx), sem("ident_ready", ctx)
            wv_turned, wvT_ready = sem("wv_turned", ctx), sem("wvT_ready", ctx)
            vo_ready = sem("vo_ready", ctx)
            weights_hi = sem("weights_hi", ctx)
            weights_lo = sem("weights_lo", ctx)
            arrived = [sem(f"arrived{n}", ctx) for n in range(2)]
            kT_zeroed = sem("kT_zeroed", ctx)
            inputs_turned = sem("inputs_turned", ctx)
            hi_ready = sem("hi_ready", ctx)
            lo_ready = sem("lo_ready", ctx)
            bias_added = sem("bias_added", ctx)
            proj_ready = sem("proj_ready", ctx)
            proj_act = sem("proj_act", ctx)
            proj_dve = sem("proj_dve", ctx)
            scores_ready = sem("scores_ready", ctx)
            top_ready = sem("top_ready", ctx)
            shifted = sem("shifted", ctx)
            exp_ready = sem("exp_ready", ctx)
            total_ready = sem("total_ready", ctx)
            inverse_ready = sem("inverse_ready", ctx)
            probs_ready = sem("probs_ready", ctx)
            probs_turned = sem("probs_turned", ctx)
            moved = [sem(f"moved{n}", ctx) for n in range(2)]
            last_turned = sem("last_turned", ctx)
            probsT_act = sem("probsT_act", ctx)
            probsT_dve = sem("probsT_dve", ctx)
            out_ready = sem("out_ready", ctx)
            out_added = sem("out_added", ctx)

            with ExitStack() as place:
                qT = [sb(f"qT{n}", [P, HP, GT], to=place) for n in range(2)]
                kT = [sb(f"kT{n}", [P, HP, 2, 4, length], to=place) for n in range(2)]
            hidden = [sb(f"hidden{n}", [P, FC, FT], to=ctx) for n in range(2)]
            hidden_hi = [sb(f"hidden_hi{n}", [P, FC, FT], FP32R, ctx) for n in range(2)]
            hidden_lo = [sb(f"hidden_lo{n}", [P, FC, FT], FP32R, ctx) for n in range(2)]
            x1_in = [blocksT[0][:, n, :, :, :].rearrange("p q t h -> p (q t h)").rearrange(
                "p (t n) -> p t n", t=4) for n in range(2)]
            x1T_hi = [wq_hi[:, n * FT:(n + 1) * FT] for n in range(2)]
            x1T_lo = [wq_lo[:, n * FT:(n + 1) * FT] for n in range(2)]
            yT = [blocksT[1][:, n, :, :, :].rearrange("p q t h -> p (q t h)") for n in range(2)]
            y = [blocksT[1][:, 2 + n, :, :, :].rearrange("p q t h -> p (q t h)").rearrange(
                "p (t n) -> p t n", t=4) for n in range(2)]
            up_bank, down_bank, in_bank, back_bank = bank[0:4], proj_bank[2], turn_bank, out_bank

            copied = sem("copied", ctx)
            x1_turned = sem("x1_turned", ctx)
            x1_hi_ready = sem("x1_hi_ready", ctx)
            x1_lo_ready = sem("x1_lo_ready", ctx)
            up_ready = sem("up_ready", ctx)
            hidden_ready = sem("hidden_ready", ctx)
            hidden_hi_ready = sem("hidden_hi_ready", ctx)
            hidden_lo_ready = sem("hidden_lo_ready", ctx)
            down_ready = sem("down_ready", ctx)
            yT_ready = sem("yT_ready", ctx)
            y_turned = sem("y_turned", ctx)
            y_ready = sem("y_ready", ctx)
            stored = [sem(f"stored{n}", ctx) for n in range(2)]

            def steps_without_qk(p):
                return 1 if isinstance(p, int) and p == PAIRS - 1 else 0

            def proj_made(p, n):
                if isinstance(p, int) and p < 0:
                    return 4 * p + 8 + n - 3
                return 8 * p + 8 + n + 1 - 4 * steps_without_qk(p)

            def taken(p, n):
                if isinstance(p, int) and p < 0:
                    return (proj_dve, p + 3) if n == 7 else (proj_act, 3 * p + 6 + n - 3)
                if n % 4 == 3:
                    return proj_dve, 2 * p + 2 + n // 4 + 1 - steps_without_qk(p)
                return proj_act, 6 * p + 6 + (n + 1 if n < 3 else n) - 3 * steps_without_qk(p)

            with nc.Block() as block:

                @block.sync
                def _(sp):
                    def load_first(g):
                        sp.dma_start(xt_in[g][:, :, :], x_rows[:, 2 * g:2 * g + 2, :]).then_inc(arrived[g], 16)
                        sp.dma_start(ct_in[g][:, :, :], c_rows[:, 2 * g:2 * g + 2, :]).then_inc(arrived[g], 16)

                    load_first(0)
                    sp.dma_start(wq_f[:, :], wq).then_inc(wq_loaded, 16)
                    sp.dma_start(wv_f[:, :], wv).then_inc(wv_loaded, 16)
                    sp.dma_start(wo_f[:, :, :], wo.rearrange("(h p) n -> p h n", p=P)).then_inc(wo_loaded, 16)
                    sp.dma_start(wk_f[:, :], wk).then_inc(wk_loaded, 16)
                    load_first(1)
                    sp.dma_start(bo_all[:, :], bo.partition_broadcast(P)).then_inc(biases_loaded, 16)
                    with nc.allow_non_contiguous_dma(reason="512 biases, once"):
                        sp.dma_start(b1_col[:, :], b1.rearrange("(c p) -> p c", p=P)).then_inc(biases_loaded, 16)
                        sp.dma_start(b2_col[:, :], b2.rearrange("(p o) -> p o", o=1)).then_inc(biases_loaded, 16)
                    sp.dma_start(w1_f[:, :], w1).then_inc(w12_loaded, 16)
                    sp.dma_start(w2_f[:, :, :], w2.rearrange("(c p) n -> p c n", p=P)).then_inc(w12_loaded, 16)
                    def load(i, n):
                        sp.wait_ge(inputs_turned, 2 * i + n - 1)
                        sp.wait_ge(bias_added, 2 * i + n - 1)
                        at = i * 4 + 2 * n
                        sp.dma_start(xt_in[n][:, :, :], x_rows[:, bass.ds(at, 2), :]).then_inc(arrived[n], 16)
                        sp.dma_start(ct_in[n][:, :, :], c_rows[:, bass.ds(at, 2), :]).then_inc(arrived[n], 16)

                    sp.wait_ge(w12_ready, 2)

                    def move(g, n):
                        sp.wait_ge(probs_turned, 4 * g + 4)
                        if not isinstance(g, int) or g > 1:
                            sp.wait_ge(out_ready, 2 * g - 2)
                        for a in range(4):
                            for b in range(4):
                                sp.dma_start(
                                    probsT[n][b * Q:(b + 1) * Q, a, :, :, :].rearrange("p q t h -> p (q t h)"),
                                    blocksT[n][a * Q:(a + 1) * Q, b, :, :, :].rearrange("p q t h -> p (q t h)")
                                ).then_inc(moved[n], 16)

                    load(1, 0)
                    load(1, 1)
                    move(0, 0)
                    with sp.Fori(2, ROUNDS) as i:
                        load(i, 0)
                        move(2 * i - 3, 1)
                        load(i, 1)
                        move(2 * i - 2, 0)
                    move(GROUPS - 3, 1)
                    move(GROUPS - 2, 0)
                    with sp.Fori(0, FSTEPS // 2) as i:
                        for n in range(2):
                            sp.wait_ge(y_ready, 2 * i + n + 1)
                            sp.dma_start(out_rows[:, bass.ds(i * 8 + 4 * n, 4), :],
                                         y[n][:, :, :]).then_inc(stored[n], 16)
                    for n in range(2):
                        sp.wait_ge(stored[n], 16 * (FSTEPS // 2))

                @block.gpsimd
                def _(pool):
                    def add_bias(i, n):
                        pool.wait_ge(arrived[n], 32 * i + 32)
                        nc.gpsimd.tensor_tensor(x1[:, bass.ds(i * 4 + 2 * n, 2), :], xt_in[n][:, :, :],
                                                bo_all[:, :].unsqueeze(1).broadcast_to([P, 2, dim]),
                                                ALU.add).then_inc(bias_added, 1)

                    def normalise(i, j):
                        p = 4 * i + j
                        for h in range(2):
                            s = slice(h * HP, (h + 1) * HP)
                            v = probs[j % 2][:, s, :]
                            pool.wait_ge(exp_ready, 2 * p + h + 1)
                            pool.wait_ge(inverse_ready, 2 * p + h + 1)
                            nc.gpsimd.tensor_tensor(
                                v, v, inverse[j % 2][:, s].unsqueeze(2).broadcast_to([P, HP, length]),
                                ALU.mult).then_inc(probs_ready, 1)

                    def copy_x1(t, n):
                        pool.wait_ge(x1_turned, t - 1)
                        nc.gpsimd.tensor_copy(x1_in[n][:, :, :], x1[:, bass.ds(t * 4, 4), :]).then_inc(copied, 1)

                    nc.gpsimd.memset(ident[:, :], 0.0).then_inc(zeroed, 1)
                    pool.wait_ge(zeroed, 1)
                    nc.gpsimd.affine_select(out=ident[:, :], in_=ident[:, :], compare_op=ALU.not_equal,
                                            fill=1.0, base=0, pattern=[[-1, P]],
                                            channel_multiplier=1).then_inc(ident_ready, 1)
                    for n in range(2):
                        nc.gpsimd.memset(kT[n][:, :, :, :, :], 0.0).then_inc(kT_zeroed, 1)
                    pool.wait_ge(biases_loaded, 48)
                    for n in range(2):
                        add_bias(0, n)
                    pool.wait_ge(w12_loaded, 32)
                    nc.gpsimd.tensor_copy(w1_hi[:, :], w1_f[:, :]).then_inc(w12_hi, 1)
                    nc.gpsimd.tensor_copy(w2_hi[:, :, :], w2_f[:, :, :]).then_inc(w12_hi, 1)
                    pool.wait_ge(w12_hi, 1)
                    nc.gpsimd.tensor_tensor(w1_lo[:, :], w1_f[:, :], w1_hi[:, :].bitcast(FP32),
                                            ALU.subtract).then_inc(w12_ready, 1)
                    pool.wait_ge(w12_hi, 2)
                    nc.gpsimd.tensor_tensor(w2_lo[:, :, :], w2_f[:, :, :], w2_hi[:, :, :].bitcast(FP32),
                                            ALU.subtract).then_inc(w12_ready, 1)
                    with pool.Fori(0, ROUNDS - 1) as i:
                        for j in range(4):
                            normalise(i, j)
                            if j % 2:
                                add_bias(i + 1, j // 2)
                    for j in range(4):
                        normalise(ROUNDS - 1, j)
                    pool.wait_ge(out_added, PAIRS)
                    with pool.Fori(0, (FSTEPS - 6) // 2) as i:
                        for n in range(2):
                            copy_x1(2 * i + n + 5, 1 - n)

                @block.tensor
                def _(pe):
                    def turn_inputs(i, n):
                        pe.wait_ge(arrived[n], 32 * i + 32)
                        pe.wait_ge(lo_ready, 2 * i + n)
                        for s, t in enumerate((xt_in[n][:, 0, :], xt_in[n][:, 1, :],
                                               ct_in[n][:, 0, :], ct_in[n][:, 1, :])):
                            last = nc.tensor.transpose(turn_bank[:, s * P:(s + 1) * P], t, ident[:, :])
                        last.then_inc(inputs_turned, 1)

                    def first_qk(which):
                        pe.wait_ge(weights_lo, which + 1)
                        pe.wait_ge(hi_ready, 1)
                        pe.wait_ge(lo_ready, 1)
                        for n in range(4):
                            if which:
                                pe.wait_ge(*taken(-2, 4 + n))
                            make_qk(0, which, n)

                    def make_qk(n, which, bank_no):
                        hi, lo = (wq_hi, wq_lo) if which == 0 else (wk_hi, wk_lo)
                        if which == 0:
                            in_hi, in_lo = xT_hi[n][:, :], xT_lo[n][:, :]
                        else:
                            in_hi, in_lo = cT_hi[n][:, :, 0:P], cT_lo[n][:, :, 0:P]
                        to = proj_bank[bank_no]
                        for h in range(2):
                            cols = slice((2 * bank_no + h) * P, (2 * bank_no + h + 1) * P)
                            o = to[:, h * GT:(h + 1) * GT]
                            o = o if which == 0 else o.rearrange("p (t n) -> p t n", t=2)
                            nc.tensor.matmul(o, hi[:, cols], in_hi, start=True, stop=False)
                            nc.tensor.matmul(o, hi[:, cols], in_lo, start=False, stop=False)
                            last = nc.tensor.matmul(o, lo[:, cols], in_hi, start=False, stop=True)
                        last.then_inc(proj_ready, 1)

                    def scores(i, j):
                        p, g = 4 * i + j, j // 2
                        for h in range(HP):
                            if h % HALF == 0 and (not isinstance(p, int) or p > 0):
                                pe.wait_ge(shifted, 2 * p - 1 + h // HALF)
                            if j % 2 == 0 and h % 2 == 0:
                                pe.wait_ge(*taken(p - 1, 4 + h // 2))
                            for b in range(2):
                                at = (j % 2) * P + b * length
                                last = nc.tensor.matmul(
                                    score_bank[h // HALF][b * length:(b + 1) * length,
                                                          (h % HALF) * P:(h % HALF + 1) * P],
                                    qT[g][:, h, at:at + length],
                                    kT[g][:, h, j % 2, 2 * b:2 * b + 2, :].rearrange("p s k -> p (s k)"),
                                    start=True, stop=True)
                            if h % HALF == HALF - 1:
                                last.then_inc(scores_ready, 1)

                    def make_cvo(i, j):
                        p, g = 4 * i + j, j // 2
                        pe.wait_ge(hi_ready, 2 * i + g + 1)
                        pe.wait_ge(lo_ready, 2 * i + g + 1)
                        for n in range(4):
                            odd, hs = n // 2, slice(4 * (n % 2), 4 * (n % 2) + 4)
                            pe.wait_ge(*taken(p - 1, n if steps_without_qk(p) else 4 + n))
                            rows = slice(odd * length, odd * length + P)
                            c_hi, c_lo = cT_hi[g][:, j % 2, rows], cT_lo[g][:, j % 2, rows]
                            w_hi = vo_hi[:, odd, hs, :].rearrange("p h n -> p (h n)")
                            w_lo = vo_lo[:, odd, hs, :].rearrange("p h n -> p (h n)")
                            nc.tensor.matmul(proj_bank[n][:, :], c_hi, w_hi, start=True, stop=False)
                            nc.tensor.matmul(proj_bank[n][:, :], c_hi, w_lo, start=False, stop=False)
                            nc.tensor.matmul(proj_bank[n][:, :], c_lo, w_hi, start=False,
                                             stop=True).then_inc(proj_ready, 1)

                    def attend(p, j):
                        if isinstance(p, int) and p >= PAIRS - 2:
                            pe.wait_ge(probsT_act, p - PAIRS + 3)
                            pe.wait_ge(probsT_dve, p - PAIRS + 3)
                        else:
                            pe.wait_ge(moved[j // 2], (p - j) * 64 + 256)
                        pe.wait_ge(*taken(p, 2))
                        pe.wait_ge(*taken(p, 3))
                        if not isinstance(p, int) or p > 0:
                            pe.wait_ge(out_added, p)
                        for h in range(HP):
                            for b in range(2):
                                last = nc.tensor.matmul(out_bank[b * length:(b + 1) * length, 0:dim],
                                                        probsT[j // 2][:, 2 * b:2 * b + 2, :, j % 2, h]
                                                        .rearrange("p a q -> p (a q)"),
                                                        cvo[j][:, b, h, :], start=h == 0, stop=h == HP - 1)
                        last.then_inc(out_ready, 1)

                    def turn_last(t, h):
                        pe.wait_ge(probs_ready, 2 * (PAIRS - 2 + t) + h + 1)
                        pe.wait_ge(*taken(PAIRS - 1, 2 * t + h))
                        for n in range(HALF):
                            at = 2 * (h * HALF + n)
                            last = nc.tensor.transpose(
                                proj_bank[2 * t + h][:, n * P:(n + 1) * P],
                                probs[t][:, at:at + 2, :].rearrange("p s k -> p (s k)"), ident[:, :])
                        last.then_inc(last_turned, 1)

                    def step(i, j, more):
                        p, g = 4 * i + j, j // 2
                        if not isinstance(p, int) or p >= 4:
                            attend(p - 4, j)
                        make_cvo(i, j)
                        if more and j % 2:
                            turn_inputs(i + 1, g)
                        scores(i, j)
                        if more or j < 2:
                            for n in range(4):
                                qk_bank(i, j, n)

                    def qk_bank(i, j, n):
                        p, g = 4 * i + j, j // 2
                        pe.wait_ge(hi_ready, 2 * i + g + 2)
                        pe.wait_ge(lo_ready, 2 * i + g + 2)
                        pe.wait_ge(*taken(p, n))
                        make_qk((g + 1) % 2, j % 2, n)

                    def turn_x1(t, n, before):
                        if isinstance(t, int):
                            pe.wait_ge(out_added, 4 * t + 4)
                        else:
                            pe.wait_ge(copied, t - 4)
                        if before:
                            pe.wait_ge(x1_lo_ready, t)
                        for s in range(4):
                            src = x1[:, 4 * t + s, :] if isinstance(t, int) else x1_in[n][:, s, :]
                            last = nc.tensor.transpose(in_bank[:, s * P:(s + 1) * P], src, ident[:, :])
                        last.then_inc(x1_turned, 1)

                    def up(t, n, before, chunks=range(FC)):
                        if isinstance(t, int) and t == 0:
                            pe.wait_ge(w12_ready, 2)
                        pe.wait_ge(x1_hi_ready, t + 1)
                        pe.wait_ge(x1_lo_ready, t + 1)
                        for c in chunks:
                            if before:
                                pe.wait_ge(hidden_ready, FC * t - FC + c + 1)
                            cols = slice(c * P, (c + 1) * P)
                            nc.tensor.matmul(up_bank[c][:, :], w1_hi[:, cols], x1T_hi[n][:, :], start=True, stop=False)
                            nc.tensor.matmul(up_bank[c][:, :], w1_hi[:, cols], x1T_lo[n][:, :], start=False, stop=False)
                            nc.tensor.matmul(up_bank[c][:, :], w1_lo[:, cols], x1T_hi[n][:, :], start=False,
                                             stop=True).then_inc(up_ready, 1)

                    def down(t, n, before):
                        if before:
                            pe.wait_ge(yT_ready, t)
                        else:
                            pe.wait_ge(probsT_act, 2)
                        for c in range(FC):
                            pe.wait_ge(hidden_hi_ready, FC * t + c + 1)
                            nc.tensor.matmul(down_bank[:, :], w2_hi[:, c, :], hidden_hi[n][:, c, :], start=c == 0, stop=False)
                            nc.tensor.matmul(down_bank[:, :], w2_lo[:, c, :], hidden_hi[n][:, c, :], start=False, stop=False)
                            pe.wait_ge(hidden_lo_ready, FC * t + c + 1)
                            last = nc.tensor.matmul(down_bank[:, :], w2_hi[:, c, :], hidden_lo[n][:, c, :],
                                                    start=False, stop=c == FC - 1)
                        last.then_inc(down_ready, 1)

                    def turn_y(t, n, before):
                        pe.wait_ge(yT_ready, t + 1)
                        if before:
                            pe.wait_ge(y_ready, t)
                        else:
                            pe.wait_ge(out_added, PAIRS)
                        for s in range(4):
                            last = nc.tensor.transpose(back_bank[:, s * P:(s + 1) * P], yT[n][:, s * P:(s + 1) * P],
                                                       ident[:, :])
                        last.then_inc(y_turned, 1)

                    pe.wait_ge(ident_ready, 1)
                    turn_inputs(0, 0)
                    pe.wait_ge(wv_loaded, 16)
                    for h in range(HP):
                        last = nc.tensor.transpose(score_bank[h // 4][:, (h % 4) * P:(h % 4 + 1) * P],
                                                   wv_f[:, h * P:(h + 1) * P], ident[:, :])
                    last.then_inc(wv_turned, 1)
                    first_qk(0)
                    pe.wait_ge(wvT_ready, 1)
                    pe.wait_ge(wo_loaded, 16)
                    pe.wait_ge(lo_ready, 1)
                    for odd in range(2):
                        r = slice(odd * d_head, (odd + 1) * d_head)
                        for h in range(HP):
                            last = nc.tensor.matmul(vo_bank[2 * odd + h // 4][:, (h % 4) * P:(h % 4 + 1) * P],
                                                    wvT[r, h, :], wo_f[r, h, :], start=True, stop=True)
                            if h % 4 == 3:
                                last.then_inc(vo_ready, 1)
                    first_qk(1)
                    pe.wait_ge(weights_lo, 6)
                    turn_inputs(0, 1)
                    pe.wait_ge(kT_zeroed, 2)
                    for j in range(4):
                        step(0, j, True)
                    with pe.Fori(1, ROUNDS - 1) as i:
                        for j in range(4):
                            step(i, j, True)
                    for j in range(4):
                        if j == 3:
                            turn_x1(0, 0, False)
                        step(ROUNDS - 1, j, False)
                    turn_last(0, 0)
                    turn_last(0, 1)
                    for c in range(2):
                        pe.wait_ge(shifted, 2 * PAIRS - 1 + c)
                        up(0, 0, False, [c])
                    pe.wait_ge(probsT_act, 1)
                    pe.wait_ge(probsT_dve, 1)
                    up(0, 0, False, range(2, FC))
                    attend(PAIRS - 4, 0)
                    turn_x1(1, 1, True)
                    turn_last(1, 0)
                    turn_last(1, 1)
                    attend(PAIRS - 3, 1)
                    up(1, 1, True, range(2))
                    attend(PAIRS - 2, 2)
                    up(1, 1, True, range(2, FC))
                    attend(PAIRS - 1, 3)
                    turn_x1(2, 0, True)
                    down(0, 0, False)
                    up(2, 0, True)
                    turn_x1(3, 1, True)
                    down(1, 1, True)
                    turn_y(0, 0, False)
                    up(3, 1, True)
                    turn_x1(4, 0, True)
                    down(2, 0, True)
                    turn_y(1, 1, True)
                    with pe.Fori(2, FSTEPS // 2 - 1) as i:
                        for n in range(2):
                            up(2 * i + n, n, True)
                            turn_x1(2 * i + n + 1, 1 - n, True)
                            down(2 * i + n - 1, 1 - n, True)
                            turn_y(2 * i + n - 2, n, True)
                    t = FSTEPS - 2
                    up(t, 0, True)
                    turn_x1(t + 1, 1, True)
                    down(t - 1, 1, True)
                    turn_y(t - 2, 0, True)
                    up(t + 1, 1, True)
                    down(t, 0, True)
                    turn_y(t - 1, 1, True)
                    down(t + 1, 1, True)
                    turn_y(t, 0, True)
                    turn_y(t + 1, 1, True)

                @block.scalar
                def _(act):
                    def round_inputs(i, n):
                        act.wait_ge(inputs_turned, 2 * i + n + 1)
                        c = turn_bank[:, GT:2 * GT].rearrange("p (t n) -> p t n", t=2)
                        nc.scalar.activation(xT_hi[n][:, :], turn_bank[:, 0:GT], ACT.Copy)
                        nc.scalar.activation(cT_hi[n][:, :, 0:P], c, ACT.Copy)
                        nc.scalar.activation(cT_hi[n][:, :, P:P + length], c[:, :, 0:length],
                                             ACT.Copy).then_inc(hi_ready, 1)

                    def take_q(n, bank_no, made):
                        act.wait_ge(proj_ready, made)
                        nc.scalar.activation(qT[n][:, 2 * bank_no:2 * bank_no + 2, :],
                                             proj_bank[bank_no][:, :].rearrange("p (h t) -> p h t", h=2),
                                             ACT.Copy).then_inc(proj_act, 1)

                    def take_k(n, bank_no, made):
                        act.wait_ge(proj_ready, made)
                        k = kT[n][:, 2 * bank_no:2 * bank_no + 2, :, :, :].rearrange("p h t s k -> p (h t) s k")
                        src = proj_bank[bank_no][:, :].rearrange("p (m s k) -> p m s k", s=2, k=length)
                        nc.scalar.activation(k[0:d_head, :, 0:4:3, :], src[0:d_head], ACT.Copy)
                        nc.scalar.activation(k[d_head:P, :, 1:3, :], src[d_head:P],
                                             ACT.Copy).then_inc(proj_act, 1)

                    def exponentials(i, j, h):
                        p = 4 * i + j
                        v = probs[j % 2][:, h * HP:(h + 1) * HP, :]
                        act.wait_ge(shifted, 2 * p + h + 1)
                        nc.scalar.activation(v, v, ACT.Exp, scale=SCALE).then_inc(exp_ready, 1)

                    def take_cvo(i, j, n):
                        p = 4 * i + j
                        act.wait_ge(proj_ready, proj_made(p, n))
                        src = proj_bank[n][:, :].rearrange("p (h n) -> p h n", h=4)
                        odd, hs = n // 2, slice(4 * (n % 2), 4 * (n % 2) + 4)
                        nc.scalar.activation(cvo[j][0:length, odd, hs, :], src[0:length], ACT.Copy)
                        nc.scalar.activation(cvo[j][length:P, 1 - odd, hs, :], src[length:P],
                                             ACT.Copy).then_inc(proj_act, 1)

                    def take_last(t):
                        act.wait_ge(last_turned, 2 * t + 1)
                        nc.scalar.activation(probsT[1][:, :, :, t, 0:HALF].rearrange("p a q h -> p h a q"),
                                             proj_bank[2 * t][:, :].rearrange("p (h a q) -> p h a q", h=HALF, q=Q),
                                             ACT.Copy).then_inc(probsT_act, 1)

                    def step(i, j, more):
                        p, g = 4 * i + j, j // 2
                        for n in range(3):
                            take_cvo(i, j, n)
                        if more and j % 2:
                            round_inputs(i + 1, g)
                        for n in ([4, 0, 5, 1, 6] if j % 2 else [4, 5, 6, 0, 1]):
                            if n < 2:
                                exponentials(i, j, n)
                            elif more or j < 2:
                                (take_k if j % 2 else take_q)((g + 1) % 2, n - 4, proj_made(p, n))

                    def round_x1(t, n):
                        act.wait_ge(x1_turned, t + 1)
                        nc.scalar.activation(x1T_hi[n][:, :], in_bank[:, :], ACT.Copy).then_inc(x1_hi_ready, 1)

                    def gelu(t, n):
                        for c in range(FC):
                            act.wait_ge(up_ready, FC * t + c + 1)
                            nc.scalar.activation(hidden[n][:, c, :], up_bank[c][:, :], ACT.Gelu,
                                                 bias=b1_col[:, c:c + 1]).then_inc(hidden_ready, 1)

                    def add_b2(t, n):
                        act.wait_ge(down_ready, t + 1)
                        nc.scalar.activation(yT[n][:, :], down_bank[:, :], ACT.Identity,
                                             bias=b2_col[:, 0:1]).then_inc(yT_ready, 1)

                    def forward(t, n, before):
                        if before:
                            act.wait_ge(hidden_lo_ready, FC * t - FC)
                        gelu(t, n)
                        round_x1(t + 1, 1 - n)
                        if before:
                            add_b2(t - 1, 1 - n)

                    round_inputs(0, 0)
                    act.wait_ge(wq_loaded, 16)
                    nc.scalar.activation(wq_hi[:, :], wq_f[:, :], ACT.Copy).then_inc(weights_hi, 1)
                    act.wait_ge(wv_turned, 1)
                    for n in range(2):
                        last = nc.scalar.activation(wvT[:, 4 * n:4 * n + 4, :], score_bank[n][:, :].rearrange(
                            "p (h n) -> p h n", h=4), ACT.Copy)
                    last.then_inc(wvT_ready, 1)
                    for n in range(3):
                        take_q(0, n, proj_made(-2, 4 + n))
                        if n == 0:
                            act.wait_ge(wk_loaded, 16)
                            nc.scalar.activation(wk_hi[:, :], wk_f[:, :], ACT.Copy).then_inc(weights_hi, 1)
                    for n in range(4):
                        act.wait_ge(vo_ready, n + 1)
                        nc.scalar.activation(vo_hi[:, n // 2, 4 * (n % 2):4 * (n % 2) + 4, :],
                                             vo_bank[n][:, :].rearrange("p (h n) -> p h n", h=4),
                                             ACT.Copy).then_inc(weights_hi, 1)
                    act.wait_ge(kT_zeroed, 2)
                    for n in range(3):
                        take_k(0, n, proj_made(-1, 4 + n))
                    round_inputs(0, 1)
                    for j in range(4):
                        step(0, j, True)
                    with act.Fori(1, ROUNDS - 1) as i:
                        for j in range(4):
                            step(i, j, True)
                    for j in range(4):
                        if j == 3:
                            round_x1(0, 0)
                        step(ROUNDS - 1, j, False)
                    take_last(0)
                    gelu(0, 0)
                    round_x1(1, 1)
                    take_last(1)
                    gelu(1, 1)
                    round_x1(2, 0)
                    add_b2(0, 0)
                    with act.Fori(1, FSTEPS // 2 - 1) as i:
                        for n in range(2):
                            forward(2 * i + n, n, True)
                    t = FSTEPS - 2
                    forward(t, 0, True)
                    act.wait_ge(hidden_lo_ready, FC * t)
                    gelu(t + 1, 1)
                    add_b2(t, 0)
                    add_b2(t + 1, 1)

                @block.vector
                def _(dve):
                    def split_inputs(i, n):
                        dve.wait_ge(hi_ready, 2 * i + n + 1)
                        c = turn_bank[:, GT:2 * GT].rearrange("p (t n) -> p t n", t=2)
                        nc.vector.tensor_tensor(xT_lo[n][:, :], turn_bank[:, 0:GT],
                                                xT_hi[n][:, :].bitcast(FP32), ALU.subtract)
                        nc.vector.tensor_tensor(cT_lo[n][:, :, 0:P], c,
                                                cT_hi[n][:, :, 0:P].bitcast(FP32), ALU.subtract)
                        nc.vector.tensor_tensor(cT_lo[n][:, :, P:P + length], c[:, :, 0:length],
                                                cT_hi[n][:, :, 0:length].bitcast(FP32),
                                                ALU.subtract).then_inc(lo_ready, 1)

                    def shift(i, j, h):
                        p = 4 * i + j
                        s = slice(h * HP, (h + 1) * HP)
                        v = score_bank[h][:, :].rearrange("p (s k) -> p s k", k=length)
                        dve.wait_ge(scores_ready, 2 * p + h + 1)
                        nc.vector.reduce_max(top[j % 2][:, s], v, AX.X).then_inc(top_ready, 1)
                        if not isinstance(p, int) or p > 1:
                            dve.wait_ge(probs_turned, 2 * p + h - 3)
                        dve.wait_ge(top_ready, 2 * p + h + 1)
                        nc.vector.tensor_tensor(probs[j % 2][:, s, :], v,
                                                top[j % 2][:, s].unsqueeze(2).broadcast_to([P, HP, length]),
                                                ALU.subtract).then_inc(shifted, 1)

                    def take_cvo(i, j):
                        p = 4 * i + j
                        dve.wait_ge(proj_ready, proj_made(p, 3))
                        src = proj_bank[3][:, :].rearrange("p (h n) -> p h n", h=4)
                        nc.vector.tensor_copy(cvo[j][0:length, 1, HALF:HP, :], src[0:length])
                        nc.vector.tensor_copy(cvo[j][length:P, 0, HALF:HP, :],
                                              src[length:P]).then_inc(proj_dve, 1)

                    def take_q(n, made):
                        dve.wait_ge(proj_ready, made)
                        nc.vector.tensor_copy(qT[n][:, HP - 2:HP, :],
                                              proj_bank[3][:, :].rearrange("p (h t) -> p h t", h=2)
                                              ).then_inc(proj_dve, 1)

                    def take_k(n, made):
                        dve.wait_ge(proj_ready, made)
                        k = kT[n][:, HP - 2:HP, :, :, :].rearrange("p h t s k -> p (h t) s k")
                        src = proj_bank[3][:, :].rearrange("p (m s k) -> p m s k", s=2, k=length)
                        nc.vector.tensor_copy(k[0:d_head, :, 0:4:3, :], src[0:d_head])
                        nc.vector.tensor_copy(k[d_head:P, :, 1:3, :], src[d_head:P]).then_inc(proj_dve, 1)

                    def turn_blocks(p, j):
                        g = j // 2
                        if not isinstance(p, int) or p >= 4:
                            dve.wait_ge(moved[g], (p - j) * 64)
                        for h in range(2):
                            hs = slice(h * HALF, (h + 1) * HALF)
                            dve.wait_ge(probs_ready, 2 * p + h + 1)
                            nc.vector.transpose(
                                blocksT[g][:, :, :, j % 2, hs].rearrange("p b q h -> p h b q"),
                                probs[j % 2][:, h * HP:(h + 1) * HP, :].rearrange(
                                    "p (h s) (c k) -> p h (s c) k", s=2, k=Q)).then_inc(probs_turned, 1)

                    def invert_sums(p, n, h):
                        s = slice(h * HP, (h + 1) * HP)
                        dve.wait_ge(exp_ready, 2 * p + h + 1)
                        nc.vector.reduce_sum(total[n][:, s], probs[n][:, s, :], AX.X).then_inc(total_ready, 1)
                        dve.wait_ge(total_ready, 2 * p + h + 1)
                        nc.vector.reciprocal(inverse[n][:, s], total[n][:, s]).then_inc(inverse_ready, 1)

                    def take_last(t):
                        dve.wait_ge(last_turned, 2 * t + 2)
                        nc.vector.tensor_copy(probsT[1][:, :, :, t, HALF:HP].rearrange("p a q h -> p h a q"),
                                              proj_bank[2 * t + 1][:, :].rearrange("p (h a q) -> p h a q", h=HALF, q=Q)
                                              ).then_inc(probsT_dve, 1)

                    def add_output(p, groups):
                        dve.wait_ge(bias_added, groups)
                        dve.wait_ge(out_ready, p + 1)
                        at = x1[:, bass.ds(p, 1), :].rearrange("p o n -> p (o n)")
                        nc.vector.tensor_tensor(at, out_bank[:, 0:dim], at, ALU.add).then_inc(out_added, 1)

                    def step(i, j, more):
                        p, g = 4 * i + j, j // 2
                        static = isinstance(p, int)
                        if not static or p > 0:
                            invert_sums(p - 1, (j + 1) % 2, 0)
                            invert_sums(p - 1, (j + 1) % 2, 1)
                        if not static or p >= 4:
                            add_output(p - 4, 2 * i + g - 1)
                        if static and p == PAIRS - 1:
                            split_x1(0, 0)
                        if not static or 0 < p < PAIRS - 1:
                            turn_blocks(p - 1, (j + 3) % 4)
                        take_cvo(i, j)
                        if more and j % 2:
                            split_inputs(i + 1, g)
                        shift(i, j, 0)
                        shift(i, j, 1)
                        if more or j < 2:
                            (take_k if j % 2 else take_q)((g + 1) % 2, proj_made(p, 7))

                    def split_x1(t, n):
                        dve.wait_ge(x1_hi_ready, t + 1)
                        nc.vector.tensor_tensor(x1T_lo[n][:, :], in_bank[:, :], x1T_hi[n][:, :].bitcast(FP32),
                                                ALU.subtract).then_inc(x1_lo_ready, 1)

                    def split_hidden(t, n, chunks):
                        for c in chunks:
                            dve.wait_ge(hidden_ready, FC * t + c + 1)
                            nc.vector.tensor_copy(hidden_hi[n][:, c, :], hidden[n][:, c, :]).then_inc(hidden_hi_ready, 1)
                            dve.wait_ge(hidden_hi_ready, FC * t + c + 1)
                            nc.vector.tensor_tensor(hidden_lo[n][:, c, :], hidden[n][:, c, :],
                                                    hidden_hi[n][:, c, :].bitcast(FP32),
                                                    ALU.subtract).then_inc(hidden_lo_ready, 1)

                    def add_x1(t, n, writes):
                        dve.wait_ge(y_turned, t + 1)
                        if writes is not None:
                            dve.wait_ge(stored[n], writes)
                        nc.vector.tensor_tensor(y[n][:, :, :], back_bank[:, :].rearrange("p (t n) -> p t n", t=4),
                                                x1[:, bass.ds(t * 4, 4), :], ALU.add).then_inc(y_ready, 1)

                    def forward(t, n, last):
                        split_hidden(t, n, range(FC - 1))
                        if not last:
                            split_x1(t + 1, 1 - n)
                        split_hidden(t, n, range(FC - 1, FC))

                    split_inputs(0, 0)
                    dve.wait_ge(weights_hi, 1)
                    nc.vector.tensor_tensor(wq_lo[:, :], wq_f[:, :], wq_hi[:, :].bitcast(FP32),
                                            ALU.subtract).then_inc(weights_lo, 1)
                    dve.wait_ge(weights_hi, 2)
                    nc.vector.tensor_tensor(wk_lo[:, :], wk_f[:, :], wk_hi[:, :].bitcast(FP32),
                                            ALU.subtract).then_inc(weights_lo, 1)
                    for n in range(4):
                        hs = slice(4 * (n % 2), 4 * (n % 2) + 4)
                        dve.wait_ge(weights_hi, 3 + n)
                        nc.vector.tensor_tensor(
                            vo_lo[:, n // 2, hs, :], vo_bank[n][:, :].rearrange("p (h n) -> p h n", h=4),
                            vo_hi[:, n // 2, hs, :].bitcast(FP32), ALU.subtract).then_inc(weights_lo, 1)
                        if n == 1:
                            take_q(0, proj_made(-2, 7))
                    dve.wait_ge(kT_zeroed, 2)
                    take_k(0, proj_made(-1, 7))
                    split_inputs(0, 1)
                    for j in range(4):
                        step(0, j, True)
                    with dve.Fori(1, ROUNDS - 1) as i:
                        for j in range(4):
                            step(i, j, True)
                    for j in range(4):
                        step(ROUNDS - 1, j, False)
                    for h in range(2):
                        invert_sums(PAIRS - 1, 1, h)
                    take_last(0)
                    split_hidden(0, 0, range(2))
                    add_output(PAIRS - 4, GROUPS)
                    split_x1(1, 1)
                    split_hidden(0, 0, range(2, FC))
                    take_last(1)
                    add_output(PAIRS - 3, GROUPS)
                    split_hidden(1, 1, range(1))
                    add_output(PAIRS - 2, GROUPS)
                    split_hidden(1, 1, range(1, 3))
                    add_output(PAIRS - 1, GROUPS)
                    split_x1(2, 0)
                    split_hidden(1, 1, range(3, FC))
                    for t in range(2, 4):
                        forward(t, t % 2, False)
                        add_x1(t - 2, t % 2, None)
                    with dve.Fori(2, FSTEPS // 2 - 1) as i:
                        for n in range(2):
                            forward(2 * i + n, n, False)
                            add_x1(2 * i + n - 2, n, 16 * i - 16)
                    for t in range(FSTEPS - 2, FSTEPS):
                        forward(t, t % 2, t == FSTEPS - 1)
                        add_x1(t - 2, t % 2, 16 * (t // 2) - 16)
                    for t in range(FSTEPS, FSTEPS + 2):
                        add_x1(t - 2, t % 2, 16 * (t // 2) - 16)


_INS = ["x", "ctx_1024", "L0_xattn_Wq", "L0_xattn_Wk", "L0_xattn_Wv", "L0_xattn_Wo", "L0_xattn_bo",
        "L0_xattn_W1", "L0_xattn_b1", "L0_xattn_W2", "L0_xattn_b2"]


def kernel(**inputs):
    import numpy as _np
    import concourse.bacc as _bacc
    from concourse import mybir as _mybir
    from concourse.bass_utils import run_bass_kernel_spmd as _run

    nc = _bacc.Bacc("TRN2", target_bir_lowering=False, num_devices=1)
    arrays, args = {}, []
    for name in _INS:
        a = _np.ascontiguousarray(inputs[name])
        arrays[f"in_{name}_dram"] = a
        args.append(nc.dram_tensor(f"in_{name}_dram", a.shape, _mybir.dt.from_np(a.dtype), kind="ExternalInput").ap())
    out = nc.dram_tensor("out_dram", inputs["x"].shape, _mybir.dt.float32, kind="ExternalOutput").ap()
    cross_attention_block(nc, *args, out)
    return _run(nc, [arrays], core_ids=[0]).results[0]["out_dram"]
```

```python
from contextlib import ExitStack

import concourse.bass as bass
from concourse import mybir

FP32 = mybir.dt.float32
FP32R = mybir.dt.float32r
ALU = mybir.AluOpType
ACT = mybir.ActivationFunctionType
AX = mybir.AxisListType


def cross_attention_block(nc, x, context, wq, wk, wv, wo, bo, w1, b1, w2, b2, out):
    sequences, length, dim = x.shape
    inner = wq.shape[1]
    ff = w1.shape[1]
    d_head = 64
    P = 128
    HP = inner // P
    FC = ff // P
    tokens = sequences * length
    PAIRS = tokens // P
    GROUPS = PAIRS // 2
    GT = 2 * P
    HALF = HP // 2
    BANK = 512
    Q = 32
    SCALE = float(d_head) ** -0.5
    ROUNDS = PAIRS // 4
    FT = 4 * P
    FSTEPS = tokens // FT

    x_rows = x.rearrange("b l d -> (b l) d").rearrange("(t p) d -> p t d", p=P)
    block_rows = [[src.rearrange("b l d -> (b l) d")[:, 32 * q:32 * q + 32]
                   .rearrange("(t a p) d -> p t a d", a=4, p=32) for q in range(4)] for src in (x, context)]
    out_rows = out.rearrange("b l d -> (b l) d").rearrange("(t p) d -> p t d", p=P)

    with ExitStack() as outer:
        def sb(name, shape, dt=FP32, to=outer):
            return to.enter_context(nc.sbuf_tensor(name, shape, dt))

        def sem(name, to=outer):
            return to.enter_context(nc.semaphore(name))

        bank = [outer.enter_context(nc.psum_tensor(f"bank{n}", [P, BANK], FP32)) for n in range(8)]

        ident = sb("ident", [P, P])
        wq_hi, wq_lo = sb("wq_hi", [P, inner], FP32R), sb("wq_lo", [P, inner], FP32R)
        wk_hi, wk_lo = sb("wk_hi", [P, inner], FP32R), sb("wk_lo", [P, inner], FP32R)
        vo_hi, vo_lo = sb("vo_hi", [P, 2, HP, dim], FP32R), sb("vo_lo", [P, 2, HP, dim], FP32R)
        w1_f, w2_f = sb("w1_f", [P, ff]), sb("w2_f", [P, FC, dim])
        bo_all = sb("bo_all", [P, dim])
        b1_col, b2_col = sb("b1_col", [P, FC]), sb("b2_col", [P, 1])
        x1 = sb("x1", [P, PAIRS, dim])

        with ExitStack() as ctx:
            blocks = [[sb(f"{of}_blocks{n}", [P, 2, 4, Q], to=ctx) for n in range(2)] for of in "xc"]
            turned = [[sb(f"{of}_turned{n}", [P, 2, P], to=ctx) for n in range(2)] for of in "xc"]
            xT_hi = [sb(f"xT_hi{n}", [P, GT], FP32R, ctx) for n in range(2)]
            xT_lo = [sb(f"xT_lo{n}", [P, GT], FP32R, ctx) for n in range(2)]
            cT_hi = [sb(f"cT_hi{n}", [P, 2, 3 * length], FP32R, ctx) for n in range(2)]
            cT_lo = [sb(f"cT_lo{n}", [P, 2, 3 * length], FP32R, ctx) for n in range(2)]
            cvo = [sb(f"cvo{n}", [P, 2, HP, dim], to=ctx) for n in range(4)]
            probs = [sb(f"probs{n}", [P, 2 * HP, length], to=ctx) for n in range(2)]
            blocksT = [sb(f"blocksT{n}", [P, 4, Q, 2, HP], to=ctx) for n in range(2)]
            probsT = [sb(f"probsT{n}", [P, 4, Q, 2, HP], to=ctx) for n in range(2)]
            wq_f, wk_f, wv_f = blocksT[0][:, 0:2], blocksT[0][:, 2:4], blocksT[1][:, 0:2]
            wo_f = blocksT[1][:, 2:4]
            wq_f, wk_f, wv_f = (w.rearrange("p a b c d -> p (a b c d)") for w in (wq_f, wk_f, wv_f))
            wo_f = wo_f.rearrange("p a b c d -> p (a b c d)").rearrange("p (h n) -> p h n", h=HP)
            wvT = [probsT[0][:, 2 * odd:2 * odd + 2].rearrange("p a b c d -> p (a b c d)")
                   .rearrange("p (h n) -> p h n", h=HP) for odd in range(2)]
            top = [sb(f"top{n}", [P, 2 * HP], to=ctx) for n in range(2)]
            total = [sb(f"total{n}", [P, 2 * HP], to=ctx) for n in range(2)]
            inverse = [sb(f"inverse{n}", [P, 2 * HP], to=ctx) for n in range(2)]

            score_bank, proj_bank, out_bank = bank[0:2], bank[2:6], bank[7]
            vo_bank = [bank[0], bank[1], bank[7], bank[6]]

            wq_loaded, wk_loaded = sem("wq_loaded", ctx), sem("wk_loaded", ctx)
            wv_loaded, wo_loaded = [sem(f"wv_loaded{n}", ctx) for n in range(2)], sem("wo_loaded", ctx)
            w12_loaded, w12_hi = sem("w12_loaded", ctx), sem("w12_hi", ctx)
            w12_ready = sem("w12_ready", ctx)
            biases_loaded = sem("biases_loaded", ctx)
            zeroed, ident_ready = sem("zeroed", ctx), sem("ident_ready", ctx)
            wv_turned = sem("wv_turned", ctx)
            wvT_padded = sem("wvT_padded", ctx)
            wvT_act, wvT_dve = sem("wvT_act", ctx), sem("wvT_dve", ctx)
            vo_ready = sem("vo_ready", ctx)
            weights_hi = sem("weights_hi", ctx)
            weights_lo = sem("weights_lo", ctx)
            arrived = [[sem(f"{of}_arrived{n}", ctx) for n in range(2)] for of in "xc"]
            x1_loaded = sem("x1_loaded", ctx)
            kT_zeroed = sem("kT_zeroed", ctx)
            inputs_turned = sem("inputs_turned", ctx)
            hi_ready = sem("hi_ready", ctx)
            lo_ready = sem("lo_ready", ctx)
            bias_added = sem("bias_added", ctx)
            proj_ready = sem("proj_ready", ctx)
            proj_act = sem("proj_act", ctx)
            proj_dve = sem("proj_dve", ctx)
            scores_ready = sem("scores_ready", ctx)
            top_ready = sem("top_ready", ctx)
            shifted = sem("shifted", ctx)
            exp_ready = sem("exp_ready", ctx)
            total_ready = sem("total_ready", ctx)
            inverse_ready = sem("inverse_ready", ctx)
            probs_ready = sem("probs_ready", ctx)
            probs_turned = sem("probs_turned", ctx)
            moved = [sem(f"moved{n}", ctx) for n in range(2)]
            last_turned = sem("last_turned", ctx)
            probsT_act = sem("probsT_act", ctx)
            probsT_dve = sem("probsT_dve", ctx)
            out_ready = sem("out_ready", ctx)
            out_added = sem("out_added", ctx)

            with ExitStack() as place:
                qT = [sb(f"qT{n}", [P, HP, GT], to=place) for n in range(2)]
                kT = [sb(f"kT{n}", [P, HP, 2, 4, length], to=place) for n in range(2)]
            hidden = [sb(f"hidden{n}", [P, FC, FT], to=ctx) for n in range(2)]
            hidden_hi = [sb(f"hidden_hi{n}", [P, FC, FT], FP32R, ctx) for n in range(2)]
            hidden_lo = [sb(f"hidden_lo{n}", [P, FC, FT], FP32R, ctx) for n in range(2)]
            x1_in = [blocksT[0][:, n, :, :, :].rearrange("p q t h -> p (q t h)").rearrange(
                "p (t n) -> p t n", t=4) for n in range(2)]
            w1_hi, w1_lo = (w[:, 0:ff] for w in (wk_hi, wk_lo))
            w2_hi, w2_lo = (w[:, ff:2 * ff].rearrange("p (c n) -> p c n", c=FC) for w in (wk_hi, wk_lo))
            x1T_hi = [wq_hi[:, n * FT:(n + 1) * FT] for n in range(2)]
            x1T_lo = [wq_lo[:, n * FT:(n + 1) * FT] for n in range(2)]
            yT = [blocksT[1][:, n, :, :, :].rearrange("p q t h -> p (q t h)") for n in range(2)]
            y = [blocksT[1][:, 2 + n, :, :, :].rearrange("p q t h -> p (q t h)").rearrange(
                "p (t n) -> p t n", t=4) for n in range(2)]
            up_bank, down_bank, in_bank, back_bank = bank[0:4], proj_bank[2], bank[6], out_bank

            copied = sem("copied", ctx)
            x1_turned = sem("x1_turned", ctx)
            x1_hi_ready = sem("x1_hi_ready", ctx)
            x1_lo_ready = sem("x1_lo_ready", ctx)
            up_ready = sem("up_ready", ctx)
            hidden_ready = sem("hidden_ready", ctx)
            hidden_hi_ready = sem("hidden_hi_ready", ctx)
            hidden_lo_ready = sem("hidden_lo_ready", ctx)
            down_ready = sem("down_ready", ctx)
            yT_ready = sem("yT_ready", ctx)
            y_turned = sem("y_turned", ctx)
            y_ready = sem("y_ready", ctx)
            stored = [sem(f"stored{n}", ctx) for n in range(2)]

            def steps_without_qk(p):
                return 1 if isinstance(p, int) and p == PAIRS - 1 else 0

            def proj_made(p, n):
                if isinstance(p, int) and p < 0:
                    return 4 * p + 8 + n - 3
                return 8 * p + 8 + n + 1 - 4 * steps_without_qk(p)

            def taken(p, n):
                if isinstance(p, int) and p < 0:
                    return (proj_dve, p + 3) if n == 7 else (proj_act, 3 * p + 6 + n - 3)
                if n % 4 == 3:
                    return proj_dve, 2 * p + 2 + n // 4 + 1 - steps_without_qk(p)
                return proj_act, 6 * p + 6 + (n + 1 if n < 3 else n) - 3 * steps_without_qk(p)

            with nc.Block() as block:

                @block.sync
                def _(sp):
                    def load_blocks(of, t, n):
                        for q in range(4):
                            sp.dma_start(blocks[of][n][q * Q:(q + 1) * Q, :, :, :],
                                         block_rows[of][q][:, bass.ds(t, 2), :, :]).then_inc(arrived[of][n], 16)

                    for n in range(2):
                        half = slice(n * inner // 2, (n + 1) * inner // 2)
                        sp.dma_start(wv_f[:, half], wv[:, half]).then_inc(wv_loaded[n], 16)
                    sp.dma_start(wo_f[:, :, :], wo.rearrange("(h p) n -> p h n", p=P)).then_inc(wo_loaded, 16)
                    load_blocks(0, 0, 0)
                    sp.dma_start(wq_f[:, :], wq).then_inc(wq_loaded, 16)
                    load_blocks(1, 0, 0)
                    sp.dma_start(wk_f[:, :], wk).then_inc(wk_loaded, 16)
                    load_blocks(0, 2, 1)
                    load_blocks(1, 2, 1)
                    sp.dma_start(bo_all[:, :], bo.partition_broadcast(P)).then_inc(biases_loaded, 16)
                    with nc.allow_non_contiguous_dma(reason="512 biases, once"):
                        sp.dma_start(b1_col[:, :], b1.rearrange("(c p) -> p c", p=P)).then_inc(biases_loaded, 16)
                        sp.dma_start(b2_col[:, :], b2.rearrange("(p o) -> p o", o=1)).then_inc(biases_loaded, 16)
                    sp.dma_start(w1_f[:, :], w1).then_inc(w12_loaded, 16)
                    sp.dma_start(w2_f[:, :, :], w2.rearrange("(c p) n -> p c n", p=P)).then_inc(w12_loaded, 16)
                    def load_x1(q):
                        ts = slice(q * PAIRS // 4, (q + 1) * PAIRS // 4)
                        sp.dma_start(x1[:, ts, :], x_rows[:, ts, :]).then_inc(x1_loaded, 16)

                    def load(i, n):
                        sp.wait_ge(inputs_turned, 4 * i + 2 * n - 2)
                        for of in range(2):
                            load_blocks(of, i * 4 + 2 * n, n)


                    def move(g, n):
                        sp.wait_ge(probs_turned, 4 * g + 4)
                        if not isinstance(g, int) or g > 1:
                            sp.wait_ge(out_ready, 2 * g - 2)
                        for a in range(4):
                            for b in range(4):
                                sp.dma_start(
                                    probsT[n][b * Q:(b + 1) * Q, a, :, :, :].rearrange("p q t h -> p (q t h)"),
                                    blocksT[n][a * Q:(a + 1) * Q, b, :, :, :].rearrange("p q t h -> p (q t h)")
                                ).then_inc(moved[n], 16)

                    load(1, 0)
                    load_x1(0)
                    load(1, 1)
                    for q in range(1, 4):
                        load_x1(q)
                    move(0, 0)
                    with sp.Fori(2, ROUNDS) as i:
                        load(i, 0)
                        move(2 * i - 3, 1)
                        load(i, 1)
                        move(2 * i - 2, 0)
                    move(GROUPS - 3, 1)
                    move(GROUPS - 2, 0)
                    with sp.Fori(0, FSTEPS // 2) as i:
                        for n in range(2):
                            sp.wait_ge(y_ready, 2 * i + n + 1)
                            sp.dma_start(out_rows[:, bass.ds(i * 8 + 4 * n, 4), :],
                                         y[n][:, :, :]).then_inc(stored[n], 16)
                    for n in range(2):
                        sp.wait_ge(stored[n], 16 * (FSTEPS // 2))

                @block.gpsimd
                def _(pool):
                    def add_bias(i, n):
                        at = x1[:, bass.ds(i * 4 + 2 * n, 2), :]
                        nc.gpsimd.tensor_tensor(at, at, bo_all[:, :].unsqueeze(1).broadcast_to([P, 2, dim]),
                                                ALU.add).then_inc(bias_added, 1)

                    def split_inputs(i, n):
                        pool.wait_ge(hi_ready, 4 * i + 2 * n + 1)
                        nc.gpsimd.tensor_tensor(xT_lo[n][:, :], turned[0][n][:, :, :].rearrange("p t n -> p (t n)"),
                                                xT_hi[n][:, :].bitcast(FP32), ALU.subtract).then_inc(lo_ready, 1)
                        pool.wait_ge(hi_ready, 4 * i + 2 * n + 2)
                        nc.gpsimd.tensor_tensor(cT_lo[n][:, :, 0:P], turned[1][n][:, :, :],
                                                cT_hi[n][:, :, 0:P].bitcast(FP32), ALU.subtract)
                        nc.gpsimd.tensor_tensor(cT_lo[n][:, :, P:P + length], turned[1][n][:, :, 0:length],
                                                cT_hi[n][:, :, 0:length].bitcast(FP32),
                                                ALU.subtract).then_inc(lo_ready, 1)

                    def normalise(i, j):
                        p = 4 * i + j
                        for h in range(2):
                            s = slice(h * HP, (h + 1) * HP)
                            v = probs[j % 2][:, s, :]
                            pool.wait_ge(exp_ready, 2 * p + h + 1)
                            pool.wait_ge(inverse_ready, 2 * p + h + 1)
                            nc.gpsimd.tensor_tensor(
                                v, v, inverse[j % 2][:, s].unsqueeze(2).broadcast_to([P, HP, length]),
                                ALU.mult).then_inc(probs_ready, 1)

                    def copy_x1(t, n):
                        pool.wait_ge(x1_turned, t - 1)
                        nc.gpsimd.tensor_copy(x1_in[n][:, :, :], x1[:, bass.ds(t * 4, 4), :]).then_inc(copied, 1)

                    nc.gpsimd.memset(ident[:, :], 0.0).then_inc(zeroed, 1)
                    pool.wait_ge(zeroed, 1)
                    nc.gpsimd.affine_select(out=ident[:, :], in_=ident[:, :], compare_op=ALU.not_equal,
                                            fill=1.0, base=0, pattern=[[-1, P]],
                                            channel_multiplier=1).then_inc(ident_ready, 1)
                    for n in range(2):
                        nc.gpsimd.memset(kT[n][:, :, :, :, :], 0.0).then_inc(kT_zeroed, 1)
                    split_inputs(0, 0)
                    split_inputs(0, 1)
                    for j in range(4):
                        if j % 2:
                            split_inputs(1, j // 2)
                        normalise(0, j)
                        if j == 1:
                            pool.wait_ge(biases_loaded, 48)
                            pool.wait_ge(x1_loaded, 64)
                        if j % 2:
                            add_bias(0, j // 2)
                    add_bias(1, 0)
                    with pool.Fori(1, ROUNDS - 1) as i:
                        for j in range(4):
                            if j % 2:
                                split_inputs(i + 1, j // 2)
                            normalise(i, j)
                            if j % 2:
                                add_bias(i + j // 2, 1 - j // 2)
                    for j in range(2):
                        normalise(ROUNDS - 1, j)
                    add_bias(ROUNDS - 1, 1)
                    pool.wait_ge(proj_ready, proj_made(PAIRS - 3, 7))
                    pool.wait_ge(w12_loaded, 32)
                    nc.gpsimd.tensor_copy(w1_hi[:, :], w1_f[:, :]).then_inc(w12_hi, 1)
                    nc.gpsimd.tensor_copy(w2_hi[:, :, :], w2_f[:, :, :]).then_inc(w12_hi, 1)
                    pool.wait_ge(w12_hi, 1)
                    nc.gpsimd.tensor_tensor(w1_lo[:, :], w1_f[:, :], w1_hi[:, :].bitcast(FP32),
                                            ALU.subtract).then_inc(w12_ready, 1)
                    pool.wait_ge(w12_hi, 2)
                    nc.gpsimd.tensor_tensor(w2_lo[:, :, :], w2_f[:, :, :], w2_hi[:, :, :].bitcast(FP32),
                                            ALU.subtract).then_inc(w12_ready, 1)
                    for j in range(2, 4):
                        normalise(ROUNDS - 1, j)
                    pool.wait_ge(out_added, PAIRS)
                    with pool.Fori(0, (FSTEPS - 6) // 2) as i:
                        for n in range(2):
                            copy_x1(2 * i + n + 5, 1 - n)

                @block.tensor
                def _(pe):
                    def first_qk(which):
                        pe.wait_ge(weights_lo, 4 if which else 1)
                        pe.wait_ge(lo_ready, 1 + which)
                        for n in range(4):
                            if which:
                                pe.wait_ge(*taken(-2, 4 + n))
                            make_qk(0, which, n)

                    def make_qk(n, which, bank_no):
                        hi, lo = (wq_hi, wq_lo) if which == 0 else (wk_hi, wk_lo)
                        if which == 0:
                            in_hi, in_lo = xT_hi[n][:, :], xT_lo[n][:, :]
                        else:
                            in_hi, in_lo = cT_hi[n][:, :, 0:P], cT_lo[n][:, :, 0:P]
                        to = proj_bank[bank_no]
                        for h in range(2):
                            cols = slice((2 * bank_no + h) * P, (2 * bank_no + h + 1) * P)
                            o = to[:, h * GT:(h + 1) * GT]
                            o = o if which == 0 else o.rearrange("p (t n) -> p t n", t=2)
                            nc.tensor.matmul(o, hi[:, cols], in_hi, start=True, stop=False)
                            nc.tensor.matmul(o, hi[:, cols], in_lo, start=False, stop=False)
                            last = nc.tensor.matmul(o, lo[:, cols], in_hi, start=False, stop=True)
                        last.then_inc(proj_ready, 1)

                    def scores(i, j):
                        p, g = 4 * i + j, j // 2
                        for h in range(HP):
                            if h % HALF == 0 and (not isinstance(p, int) or p > 0):
                                pe.wait_ge(shifted, 2 * p - 1 + h // HALF)
                            if j % 2 == 0 and h % 2 == 0:
                                pe.wait_ge(*taken(p - 1, 4 + h // 2))
                            for b in range(2):
                                at = (j % 2) * P + b * length
                                last = nc.tensor.matmul(
                                    score_bank[h // HALF][b * length:(b + 1) * length,
                                                          (h % HALF) * P:(h % HALF + 1) * P],
                                    qT[g][:, h, at:at + length],
                                    kT[g][:, h, j % 2, 2 * b:2 * b + 2, :].rearrange("p s k -> p (s k)"),
                                    start=True, stop=True)
                            if h % HALF == HALF - 1:
                                last.then_inc(scores_ready, 1)

                    def make_cvo(i, j):
                        p, g = 4 * i + j, j // 2
                        pe.wait_ge(lo_ready, 4 * i + 2 * g + 2)
                        for n in range(4):
                            odd, hs = n // 2, slice(4 * (n % 2), 4 * (n % 2) + 4)
                            pe.wait_ge(*taken(p - 1, n if steps_without_qk(p) else 4 + n))
                            rows = slice(odd * length, odd * length + P)
                            c_hi, c_lo = cT_hi[g][:, j % 2, rows], cT_lo[g][:, j % 2, rows]
                            w_hi = vo_hi[:, odd, hs, :].rearrange("p h n -> p (h n)")
                            w_lo = vo_lo[:, odd, hs, :].rearrange("p h n -> p (h n)")
                            nc.tensor.matmul(proj_bank[n][:, :], c_hi, w_hi, start=True, stop=False)
                            nc.tensor.matmul(proj_bank[n][:, :], c_hi, w_lo, start=False, stop=False)
                            nc.tensor.matmul(proj_bank[n][:, :], c_lo, w_hi, start=False,
                                             stop=True).then_inc(proj_ready, 1)

                    def attend(p, j):
                        if isinstance(p, int) and p >= PAIRS - 2:
                            pe.wait_ge(probsT_act, p - PAIRS + 3)
                            pe.wait_ge(probsT_dve, p - PAIRS + 3)
                        else:
                            pe.wait_ge(moved[j // 2], (p - j) * 64 + 256)
                        pe.wait_ge(*taken(p, 2))
                        pe.wait_ge(*taken(p, 3))
                        if not isinstance(p, int) or p > 0:
                            pe.wait_ge(out_added, p)
                        for h in range(HP):
                            for b in range(2):
                                last = nc.tensor.matmul(out_bank[b * length:(b + 1) * length, 0:dim],
                                                        probsT[j // 2][:, 2 * b:2 * b + 2, :, j % 2, h]
                                                        .rearrange("p a q -> p (a q)"),
                                                        cvo[j][:, b, h, :], start=h == 0, stop=h == HP - 1)
                        last.then_inc(out_ready, 1)

                    def turn_last(t, h):
                        pe.wait_ge(probs_ready, 2 * (PAIRS - 2 + t) + h + 1)
                        pe.wait_ge(*taken(PAIRS - 1, 2 * t + h))
                        for n in range(HALF):
                            at = 2 * (h * HALF + n)
                            last = nc.tensor.transpose(
                                proj_bank[2 * t + h][:, n * P:(n + 1) * P],
                                probs[t][:, at:at + 2, :].rearrange("p s k -> p (s k)"), ident[:, :])
                        last.then_inc(last_turned, 1)

                    def step(i, j, more):
                        p, g = 4 * i + j, j // 2
                        if not isinstance(p, int) or p >= 4:
                            attend(p - 4, j)
                        make_cvo(i, j)
                        scores(i, j)
                        if more or j < 2:
                            for n in range(4):
                                qk_bank(i, j, n)

                    def qk_bank(i, j, n):
                        p, g = 4 * i + j, j // 2
                        pe.wait_ge(lo_ready, 4 * i + 2 * g + 3 + j % 2)
                        pe.wait_ge(*taken(p, n))
                        make_qk((g + 1) % 2, j % 2, n)

                    def turn_x1(t, n, before):
                        if isinstance(t, int):
                            pe.wait_ge(out_added, 4 * t + 4)
                        else:
                            pe.wait_ge(copied, t - 4)
                        if before:
                            pe.wait_ge(x1_lo_ready, t)
                        for s in range(4):
                            src = x1[:, 4 * t + s, :] if isinstance(t, int) else x1_in[n][:, s, :]
                            last = nc.tensor.transpose(in_bank[:, s * P:(s + 1) * P], src, ident[:, :])
                        last.then_inc(x1_turned, 1)

                    def up(t, n, before, chunks=range(FC)):
                        if isinstance(t, int) and t == 0:
                            pe.wait_ge(w12_ready, 2)
                        pe.wait_ge(x1_hi_ready, t + 1)
                        pe.wait_ge(x1_lo_ready, t + 1)
                        for c in chunks:
                            if before:
                                pe.wait_ge(hidden_ready, FC * t - FC + c + 1)
                            cols = slice(c * P, (c + 1) * P)
                            nc.tensor.matmul(up_bank[c][:, :], w1_hi[:, cols], x1T_hi[n][:, :], start=True, stop=False)
                            nc.tensor.matmul(up_bank[c][:, :], w1_hi[:, cols], x1T_lo[n][:, :], start=False, stop=False)
                            nc.tensor.matmul(up_bank[c][:, :], w1_lo[:, cols], x1T_hi[n][:, :], start=False,
                                             stop=True).then_inc(up_ready, 1)

                    def down(t, n, before):
                        if before:
                            pe.wait_ge(yT_ready, t)
                        else:
                            pe.wait_ge(probsT_act, 2)
                        for c in range(FC):
                            pe.wait_ge(hidden_hi_ready, FC * t + c + 1)
                            nc.tensor.matmul(down_bank[:, :], w2_hi[:, c, :], hidden_hi[n][:, c, :], start=c == 0, stop=False)
                            nc.tensor.matmul(down_bank[:, :], w2_lo[:, c, :], hidden_hi[n][:, c, :], start=False, stop=False)
                            pe.wait_ge(hidden_lo_ready, FC * t + c + 1)
                            last = nc.tensor.matmul(down_bank[:, :], w2_hi[:, c, :], hidden_lo[n][:, c, :],
                                                    start=False, stop=c == FC - 1)
                        last.then_inc(down_ready, 1)

                    def turn_y(t, n, before):
                        pe.wait_ge(yT_ready, t + 1)
                        if before:
                            pe.wait_ge(y_ready, t)
                        else:
                            pe.wait_ge(out_added, PAIRS)
                        for s in range(4):
                            last = nc.tensor.transpose(back_bank[:, s * P:(s + 1) * P], yT[n][:, s * P:(s + 1) * P],
                                                       ident[:, :])
                        last.then_inc(y_turned, 1)

                    pe.wait_ge(ident_ready, 1)
                    for h in range(HP):
                        if h % 4 == 0:
                            pe.wait_ge(wv_loaded[h // 4], 16)
                        last = nc.tensor.transpose(score_bank[h // 4][:, (h % 4) * P:(h % 4 + 1) * P],
                                                   wv_f[:, h * P:(h + 1) * P], ident[:, :])
                        if h % 4 == 3:
                            last.then_inc(wv_turned, 1)
                    pe.wait_ge(wvT_padded, 2)
                    pe.wait_ge(wo_loaded, 16)
                    for odd in range(2):
                        for h in range(HP):
                            if odd == 0 and h % 4 == 0:
                                pe.wait_ge(*((wvT_act, 1) if h == 0 else (wvT_dve, 1)))
                            last = nc.tensor.matmul(vo_bank[2 * odd + h // 4][:, (h % 4) * P:(h % 4 + 1) * P],
                                                    wvT[odd][:, h, :], wo_f[:, h, :], start=True, stop=True)
                            if h % 4 == 3:
                                last.then_inc(vo_ready, 1)
                    first_qk(0)
                    first_qk(1)
                    pe.wait_ge(weights_lo, 6)
                    pe.wait_ge(kT_zeroed, 2)
                    for j in range(4):
                        step(0, j, True)
                    with pe.Fori(1, ROUNDS - 1) as i:
                        for j in range(4):
                            step(i, j, True)
                    for j in range(4):
                        if j == 3:
                            turn_x1(0, 0, False)
                        step(ROUNDS - 1, j, False)
                    turn_last(0, 0)
                    turn_last(0, 1)
                    for c in range(2):
                        pe.wait_ge(shifted, 2 * PAIRS - 1 + c)
                        up(0, 0, False, [c])
                    pe.wait_ge(probsT_act, 1)
                    pe.wait_ge(probsT_dve, 1)
                    up(0, 0, False, range(2, FC))
                    attend(PAIRS - 4, 0)
                    turn_x1(1, 1, True)
                    turn_last(1, 0)
                    turn_last(1, 1)
                    attend(PAIRS - 3, 1)
                    up(1, 1, True, range(2))
                    attend(PAIRS - 2, 2)
                    up(1, 1, True, range(2, FC))
                    attend(PAIRS - 1, 3)
                    turn_x1(2, 0, True)
                    down(0, 0, False)
                    up(2, 0, True)
                    turn_x1(3, 1, True)
                    down(1, 1, True)
                    turn_y(0, 0, False)
                    up(3, 1, True)
                    turn_x1(4, 0, True)
                    down(2, 0, True)
                    turn_y(1, 1, True)
                    with pe.Fori(2, FSTEPS // 2 - 1) as i:
                        for n in range(2):
                            up(2 * i + n, n, True)
                            turn_x1(2 * i + n + 1, 1 - n, True)
                            down(2 * i + n - 1, 1 - n, True)
                            turn_y(2 * i + n - 2, n, True)
                    t = FSTEPS - 2
                    up(t, 0, True)
                    turn_x1(t + 1, 1, True)
                    down(t - 1, 1, True)
                    turn_y(t - 2, 0, True)
                    up(t + 1, 1, True)
                    down(t, 0, True)
                    turn_y(t - 1, 1, True)
                    down(t + 1, 1, True)
                    turn_y(t, 0, True)
                    turn_y(t + 1, 1, True)

                @block.scalar
                def _(act):
                    def round_inputs(of, i, n):
                        act.wait_ge(inputs_turned, 4 * i + 2 * n + 1 + of)
                        t = turned[of][n]
                        if of == 0:
                            nc.scalar.activation(xT_hi[n][:, :], t[:, :, :].rearrange("p t n -> p (t n)"),
                                                 ACT.Copy).then_inc(hi_ready, 1)
                        else:
                            nc.scalar.activation(cT_hi[n][:, :, 0:P], t[:, :, :], ACT.Copy)
                            nc.scalar.activation(cT_hi[n][:, :, P:P + length], t[:, :, 0:length],
                                                 ACT.Copy).then_inc(hi_ready, 1)

                    def take_q(n, bank_no, made):
                        act.wait_ge(proj_ready, made)
                        nc.scalar.activation(qT[n][:, 2 * bank_no:2 * bank_no + 2, :],
                                             proj_bank[bank_no][:, :].rearrange("p (h t) -> p h t", h=2),
                                             ACT.Copy).then_inc(proj_act, 1)

                    def take_k(n, bank_no, made):
                        act.wait_ge(proj_ready, made)
                        k = kT[n][:, 2 * bank_no:2 * bank_no + 2, :, :, :].rearrange("p h t s k -> p (h t) s k")
                        src = proj_bank[bank_no][:, :].rearrange("p (m s k) -> p m s k", s=2, k=length)
                        nc.scalar.activation(k[0:d_head, :, 0:4:3, :], src[0:d_head], ACT.Copy)
                        nc.scalar.activation(k[d_head:P, :, 1:3, :], src[d_head:P],
                                             ACT.Copy).then_inc(proj_act, 1)

                    def exponentials(i, j, h):
                        p = 4 * i + j
                        v = probs[j % 2][:, h * HP:(h + 1) * HP, :]
                        act.wait_ge(shifted, 2 * p + h + 1)
                        nc.scalar.activation(v, v, ACT.Exp, scale=SCALE).then_inc(exp_ready, 1)

                    def take_cvo(i, j, n):
                        p = 4 * i + j
                        act.wait_ge(proj_ready, proj_made(p, n))
                        src = proj_bank[n][:, :].rearrange("p (h n) -> p h n", h=4)
                        odd, hs = n // 2, slice(4 * (n % 2), 4 * (n % 2) + 4)
                        nc.scalar.activation(cvo[j][0:length, odd, hs, :], src[0:length], ACT.Copy)
                        nc.scalar.activation(cvo[j][length:P, 1 - odd, hs, :], src[length:P],
                                             ACT.Copy).then_inc(proj_act, 1)

                    def take_last(t):
                        act.wait_ge(last_turned, 2 * t + 1)
                        nc.scalar.activation(probsT[1][:, :, :, t, 0:HALF].rearrange("p a q h -> p h a q"),
                                             proj_bank[2 * t][:, :].rearrange("p (h a q) -> p h a q", h=HALF, q=Q),
                                             ACT.Copy).then_inc(probsT_act, 1)

                    def step(i, j, more):
                        p, g = 4 * i + j, j // 2
                        for n in range(3):
                            take_cvo(i, j, n)
                        if more and j % 2:
                            act.wait_ge(proj_ready, proj_made(p, 3))
                            for of in range(2):
                                round_inputs(of, i + 1, g)
                        for n in ([4, 0, 5, 1, 6] if j % 2 else [4, 5, 6, 0, 1]):
                            if n < 2:
                                exponentials(i, j, n)
                            elif more or j < 2:
                                (take_k if j % 2 else take_q)((g + 1) % 2, n - 4, proj_made(p, n))

                    def round_x1(t, n):
                        act.wait_ge(x1_turned, t + 1)
                        nc.scalar.activation(x1T_hi[n][:, :], in_bank[:, :], ACT.Copy).then_inc(x1_hi_ready, 1)

                    def gelu(t, n):
                        for c in range(FC):
                            act.wait_ge(up_ready, FC * t + c + 1)
                            nc.scalar.activation(hidden[n][:, c, :], up_bank[c][:, :], ACT.Gelu,
                                                 bias=b1_col[:, c:c + 1]).then_inc(hidden_ready, 1)

                    def add_b2(t, n):
                        act.wait_ge(down_ready, t + 1)
                        nc.scalar.activation(yT[n][:, :], down_bank[:, :], ACT.Identity,
                                             bias=b2_col[:, 0:1]).then_inc(yT_ready, 1)

                    def forward(t, n, before):
                        if before:
                            act.wait_ge(hidden_lo_ready, FC * t - FC)
                        gelu(t, n)
                        round_x1(t + 1, 1 - n)
                        if before:
                            add_b2(t - 1, 1 - n)

                    def round_vo(n):
                        act.wait_ge(vo_ready, n + 1)
                        nc.scalar.activation(vo_hi[:, n // 2, 4 * (n % 2):4 * (n % 2) + 4, :],
                                             vo_bank[n][:, :].rearrange("p (h n) -> p h n", h=4),
                                             ACT.Copy).then_inc(weights_hi, 1)

                    act.wait_ge(wv_turned, 1)
                    src = score_bank[0][:, :].rearrange("p (h n) -> p h n", h=4)
                    nc.scalar.activation(wvT[0][0:d_head, 0:4, :], src[0:d_head], ACT.Copy)
                    nc.scalar.activation(wvT[1][d_head:P, 0:4, :], src[d_head:P], ACT.Copy).then_inc(wvT_act, 1)
                    round_inputs(0, 0, 0)
                    act.wait_ge(wq_loaded, 16)
                    nc.scalar.activation(wq_hi[:, :], wq_f[:, :], ACT.Copy).then_inc(weights_hi, 1)
                    round_vo(0)
                    round_vo(1)
                    act.wait_ge(wk_loaded, 16)
                    nc.scalar.activation(wk_hi[:, :], wk_f[:, :], ACT.Copy).then_inc(weights_hi, 1)
                    round_inputs(1, 0, 0)
                    round_vo(2)
                    round_vo(3)
                    for n in range(3):
                        take_q(0, n, proj_made(-2, 4 + n))
                    act.wait_ge(kT_zeroed, 2)
                    for n in range(3):
                        take_k(0, n, proj_made(-1, 4 + n))
                    round_inputs(0, 0, 1)
                    round_inputs(1, 0, 1)
                    for j in range(4):
                        step(0, j, True)
                    with act.Fori(1, ROUNDS - 1) as i:
                        for j in range(4):
                            step(i, j, True)
                    for j in range(4):
                        if j == 3:
                            round_x1(0, 0)
                        step(ROUNDS - 1, j, False)
                    take_last(0)
                    gelu(0, 0)
                    round_x1(1, 1)
                    take_last(1)
                    gelu(1, 1)
                    round_x1(2, 0)
                    add_b2(0, 0)
                    with act.Fori(1, FSTEPS // 2 - 1) as i:
                        for n in range(2):
                            forward(2 * i + n, n, True)
                    t = FSTEPS - 2
                    forward(t, 0, True)
                    act.wait_ge(hidden_lo_ready, FC * t)
                    gelu(t + 1, 1)
                    add_b2(t, 0)
                    add_b2(t + 1, 1)

                @block.vector
                def _(dve):
                    def turn_inputs(of, i, n):
                        dve.wait_ge(arrived[of][n], 64 * i + 64)
                        if not isinstance(i, int) or i > 0:
                            dve.wait_ge(lo_ready, 4 * i + 2 * n - 2)
                        nc.vector.transpose(turned[of][n][:, :, :].rearrange("p t n -> p (t n)"),
                                            blocks[of][n][:, :, :, :].rearrange("p t a n -> p (t a n)")
                                            ).then_inc(inputs_turned, 1)

                    def shift(i, j, h):
                        p = 4 * i + j
                        s = slice(h * HP, (h + 1) * HP)
                        v = score_bank[h][:, :].rearrange("p (s k) -> p s k", k=length)
                        dve.wait_ge(scores_ready, 2 * p + h + 1)
                        nc.vector.reduce_max(top[j % 2][:, s], v, AX.X).then_inc(top_ready, 1)
                        if not isinstance(p, int) or p > 1:
                            dve.wait_ge(probs_turned, 2 * p + h - 3)
                        dve.wait_ge(top_ready, 2 * p + h + 1)
                        nc.vector.tensor_tensor(probs[j % 2][:, s, :], v,
                                                top[j % 2][:, s].unsqueeze(2).broadcast_to([P, HP, length]),
                                                ALU.subtract).then_inc(shifted, 1)

                    def take_cvo(i, j):
                        p = 4 * i + j
                        dve.wait_ge(proj_ready, proj_made(p, 3))
                        src = proj_bank[3][:, :].rearrange("p (h n) -> p h n", h=4)
                        nc.vector.tensor_copy(cvo[j][0:length, 1, HALF:HP, :], src[0:length])
                        nc.vector.tensor_copy(cvo[j][length:P, 0, HALF:HP, :],
                                              src[length:P]).then_inc(proj_dve, 1)

                    def take_q(n, made):
                        dve.wait_ge(proj_ready, made)
                        nc.vector.tensor_copy(qT[n][:, HP - 2:HP, :],
                                              proj_bank[3][:, :].rearrange("p (h t) -> p h t", h=2)
                                              ).then_inc(proj_dve, 1)

                    def take_k(n, made):
                        dve.wait_ge(proj_ready, made)
                        k = kT[n][:, HP - 2:HP, :, :, :].rearrange("p h t s k -> p (h t) s k")
                        src = proj_bank[3][:, :].rearrange("p (m s k) -> p m s k", s=2, k=length)
                        nc.vector.tensor_copy(k[0:d_head, :, 0:4:3, :], src[0:d_head])
                        nc.vector.tensor_copy(k[d_head:P, :, 1:3, :], src[d_head:P]).then_inc(proj_dve, 1)

                    def turn_blocks(p, j):
                        g = j // 2
                        if not isinstance(p, int) or p >= 4:
                            dve.wait_ge(moved[g], (p - j) * 64)
                        for h in range(2):
                            hs = slice(h * HALF, (h + 1) * HALF)
                            dve.wait_ge(probs_ready, 2 * p + h + 1)
                            nc.vector.transpose(
                                blocksT[g][:, :, :, j % 2, hs].rearrange("p b q h -> p h b q"),
                                probs[j % 2][:, h * HP:(h + 1) * HP, :].rearrange(
                                    "p (h s) (c k) -> p h (s c) k", s=2, k=Q)).then_inc(probs_turned, 1)

                    def invert_sums(p, n, h):
                        s = slice(h * HP, (h + 1) * HP)
                        dve.wait_ge(exp_ready, 2 * p + h + 1)
                        nc.vector.reduce_sum(total[n][:, s], probs[n][:, s, :], AX.X).then_inc(total_ready, 1)
                        dve.wait_ge(total_ready, 2 * p + h + 1)
                        nc.vector.reciprocal(inverse[n][:, s], total[n][:, s]).then_inc(inverse_ready, 1)

                    def take_last(t):
                        dve.wait_ge(last_turned, 2 * t + 2)
                        nc.vector.tensor_copy(probsT[1][:, :, :, t, HALF:HP].rearrange("p a q h -> p h a q"),
                                              proj_bank[2 * t + 1][:, :].rearrange("p (h a q) -> p h a q", h=HALF, q=Q)
                                              ).then_inc(probsT_dve, 1)

                    def add_output(p, groups):
                        dve.wait_ge(bias_added, groups)
                        dve.wait_ge(out_ready, p + 1)
                        at = x1[:, bass.ds(p, 1), :].rearrange("p o n -> p (o n)")
                        nc.vector.tensor_tensor(at, out_bank[:, 0:dim], at, ALU.add).then_inc(out_added, 1)

                    def step(i, j, more):
                        p, g = 4 * i + j, j // 2
                        static = isinstance(p, int)
                        if more and j % 2:
                            for of in range(2):
                                turn_inputs(of, i + 1, g)
                        if not static or p > 0:
                            invert_sums(p - 1, (j + 1) % 2, 0)
                            invert_sums(p - 1, (j + 1) % 2, 1)
                        if not static or p >= 4:
                            add_output(p - 4, 2 * i + g - 1)
                        if static and p == PAIRS - 1:
                            split_x1(0, 0)
                        if not static or 0 < p < PAIRS - 1:
                            turn_blocks(p - 1, (j + 3) % 4)
                        take_cvo(i, j)
                        shift(i, j, 0)
                        shift(i, j, 1)
                        if more or j < 2:
                            (take_k if j % 2 else take_q)((g + 1) % 2, proj_made(p, 7))

                    def split_x1(t, n):
                        dve.wait_ge(x1_hi_ready, t + 1)
                        nc.vector.tensor_tensor(x1T_lo[n][:, :], in_bank[:, :], x1T_hi[n][:, :].bitcast(FP32),
                                                ALU.subtract).then_inc(x1_lo_ready, 1)

                    def split_hidden(t, n, chunks):
                        for c in chunks:
                            dve.wait_ge(hidden_ready, FC * t + c + 1)
                            nc.vector.tensor_copy(hidden_hi[n][:, c, :], hidden[n][:, c, :]).then_inc(hidden_hi_ready, 1)
                            dve.wait_ge(hidden_hi_ready, FC * t + c + 1)
                            nc.vector.tensor_tensor(hidden_lo[n][:, c, :], hidden[n][:, c, :],
                                                    hidden_hi[n][:, c, :].bitcast(FP32),
                                                    ALU.subtract).then_inc(hidden_lo_ready, 1)

                    def add_x1(t, n, writes):
                        dve.wait_ge(y_turned, t + 1)
                        if writes is not None:
                            dve.wait_ge(stored[n], writes)
                        nc.vector.tensor_tensor(y[n][:, :, :], back_bank[:, :].rearrange("p (t n) -> p t n", t=4),
                                                x1[:, bass.ds(t * 4, 4), :], ALU.add).then_inc(y_ready, 1)

                    def forward(t, n, last):
                        split_hidden(t, n, range(FC - 1))
                        if not last:
                            split_x1(t + 1, 1 - n)
                        split_hidden(t, n, range(FC - 1, FC))

                    def split_vo(n):
                        hs = slice(4 * (n % 2), 4 * (n % 2) + 4)
                        nc.vector.tensor_tensor(
                            vo_lo[:, n // 2, hs, :], vo_bank[n][:, :].rearrange("p (h n) -> p h n", h=4),
                            vo_hi[:, n // 2, hs, :].bitcast(FP32), ALU.subtract).then_inc(weights_lo, 1)

                    nc.vector.memset(wvT[0][d_head:P, :, :], 0.0).then_inc(wvT_padded, 1)
                    nc.vector.memset(wvT[1][0:d_head, :, :], 0.0).then_inc(wvT_padded, 1)
                    dve.wait_ge(wv_turned, 2)
                    src = score_bank[1][:, :].rearrange("p (h n) -> p h n", h=4)
                    nc.vector.tensor_copy(wvT[0][0:d_head, 4:8, :], src[0:d_head])
                    nc.vector.tensor_copy(wvT[1][d_head:P, 4:8, :], src[d_head:P]).then_inc(wvT_dve, 1)
                    turn_inputs(0, 0, 0)
                    dve.wait_ge(weights_hi, 1)
                    nc.vector.tensor_tensor(wq_lo[:, :], wq_f[:, :], wq_hi[:, :].bitcast(FP32),
                                            ALU.subtract).then_inc(weights_lo, 1)
                    turn_inputs(1, 0, 0)
                    for n in range(2):
                        dve.wait_ge(weights_hi, 2 + n)
                        split_vo(n)
                    dve.wait_ge(weights_hi, 4)
                    nc.vector.tensor_tensor(wk_lo[:, :], wk_f[:, :], wk_hi[:, :].bitcast(FP32),
                                            ALU.subtract).then_inc(weights_lo, 1)
                    for n in range(2, 4):
                        dve.wait_ge(weights_hi, 3 + n)
                        split_vo(n)
                    take_q(0, proj_made(-2, 7))
                    dve.wait_ge(kT_zeroed, 2)
                    take_k(0, proj_made(-1, 7))
                    turn_inputs(0, 0, 1)
                    turn_inputs(1, 0, 1)
                    for j in range(4):
                        step(0, j, True)
                    with dve.Fori(1, ROUNDS - 1) as i:
                        for j in range(4):
                            step(i, j, True)
                    for j in range(4):
                        step(ROUNDS - 1, j, False)
                    for h in range(2):
                        invert_sums(PAIRS - 1, 1, h)
                    take_last(0)
                    split_hidden(0, 0, range(2))
                    add_output(PAIRS - 4, GROUPS)
                    split_x1(1, 1)
                    split_hidden(0, 0, range(2, FC))
                    take_last(1)
                    add_output(PAIRS - 3, GROUPS)
                    split_hidden(1, 1, range(1))
                    add_output(PAIRS - 2, GROUPS)
                    split_hidden(1, 1, range(1, 3))
                    add_output(PAIRS - 1, GROUPS)
                    split_x1(2, 0)
                    split_hidden(1, 1, range(3, FC))
                    for t in range(2, 4):
                        forward(t, t % 2, False)
                        add_x1(t - 2, t % 2, None)
                    with dve.Fori(2, FSTEPS // 2 - 1) as i:
                        for n in range(2):
                            forward(2 * i + n, n, False)
                            add_x1(2 * i + n - 2, n, 16 * i - 16)
                    for t in range(FSTEPS - 2, FSTEPS):
                        forward(t, t % 2, t == FSTEPS - 1)
                        add_x1(t - 2, t % 2, 16 * (t // 2) - 16)
                    for t in range(FSTEPS, FSTEPS + 2):
                        add_x1(t - 2, t % 2, 16 * (t // 2) - 16)


_INS = ["x", "ctx_1024", "L0_xattn_Wq", "L0_xattn_Wk", "L0_xattn_Wv", "L0_xattn_Wo", "L0_xattn_bo",
        "L0_xattn_W1", "L0_xattn_b1", "L0_xattn_W2", "L0_xattn_b2"]


def kernel(**inputs):
    import numpy as _np
    import concourse.bacc as _bacc
    from concourse import mybir as _mybir
    from concourse.bass_utils import run_bass_kernel_spmd as _run

    nc = _bacc.Bacc("TRN2", target_bir_lowering=False, num_devices=1)
    arrays, args = {}, []
    for name in _INS:
        a = _np.ascontiguousarray(inputs[name])
        arrays[f"in_{name}_dram"] = a
        args.append(nc.dram_tensor(f"in_{name}_dram", a.shape, _mybir.dt.from_np(a.dtype), kind="ExternalInput").ap())
    out = nc.dram_tensor("out_dram", inputs["x"].shape, _mybir.dt.float32, kind="ExternalOutput").ap()
    cross_attention_block(nc, *args, out)
    return _run(nc, [arrays], core_ids=[0]).results[0]["out_dram"]
```

```python
from contextlib import ExitStack

import concourse.bass as bass
from concourse import mybir

FP32 = mybir.dt.float32
FP32R = mybir.dt.float32r
ALU = mybir.AluOpType
ACT = mybir.ActivationFunctionType
AX = mybir.AxisListType


def cross_attention_block(nc, x, context, wq, wk, wv, wo, bo, w1, b1, w2, b2, out):
    sequences, length, dim = x.shape
    inner = wq.shape[1]
    ff = w1.shape[1]
    d_head = 64
    P = 128
    HP = inner // P
    FC = ff // P
    tokens = sequences * length
    PAIRS = tokens // P
    GROUPS = PAIRS // 2
    GT = 2 * P
    HALF = HP // 2
    BANK = 512
    Q = 32
    SCALE = float(d_head) ** -0.5
    ROUNDS = PAIRS // 4
    FT = 4 * P
    FSTEPS = tokens // FT

    x_rows = x.rearrange("b l d -> (b l) d").rearrange("(t p) d -> p t d", p=P)
    block_rows = [[src.rearrange("b l d -> (b l) d")[:, Q * q:Q * (q + 1)]
                   .rearrange("(t a p) d -> p t a d", a=4, p=Q) for q in range(4)] for src in (x, context)]
    out_rows = out.rearrange("b l d -> (b l) d").rearrange("(t p) d -> p t d", p=P)

    with ExitStack() as outer:
        def sb(name, shape, dt=FP32, to=outer):
            return to.enter_context(nc.sbuf_tensor(name, shape, dt))

        def sem(name, to=outer):
            return to.enter_context(nc.semaphore(name))

        bank = [outer.enter_context(nc.psum_tensor(f"bank{n}", [P, BANK], FP32)) for n in range(8)]

        ident = sb("ident", [P, P])
        m_hi, m_lo = sb("m_hi", [P, HP, 2, dim], FP32R), sb("m_lo", [P, HP, 2, dim], FP32R)
        vo_hi, vo_lo = sb("vo_hi", [P, 2, HP, dim], FP32R), sb("vo_lo", [P, 2, HP, dim], FP32R)
        w1_f, w2_f = sb("w1_f", [P, ff]), sb("w2_f", [P, FC, dim])
        bo_all = sb("bo_all", [P, dim])
        b1_col, b2_col = sb("b1_col", [P, FC]), sb("b2_col", [P, 1])
        x1 = sb("x1", [P, PAIRS, dim])

        with ExitStack() as ctx:
            blocks = [[sb(f"{of}_blocks{n}", [P, 2, 4, Q], to=ctx) for n in range(2)] for of in "xc"]
            turned = [[sb(f"{of}_turned{n}", [P, 2, P], to=ctx) for n in range(2)] for of in "xc"]
            cT_hi = [sb(f"cT_hi{n}", [P, 2, 3 * length], FP32R, ctx) for n in range(2)]
            cT_lo = [sb(f"cT_lo{n}", [P, 2, 3 * length], FP32R, ctx) for n in range(2)]
            cvo = [sb(f"cvo{n}", [P, 2, HP, dim], to=ctx) for n in range(4)]
            probs = [sb(f"probs{n}", [P, 2 * HP, length], to=ctx) for n in range(2)]
            blocksT = [sb(f"blocksT{n}", [P, 4, Q, 2, HP], to=ctx) for n in range(2)]
            probsT = [sb(f"probsT{n}", [P, 4, Q, 2, HP], to=ctx) for n in range(2)]
            wq_f, wk_f, wv_f = blocksT[0][:, 0:2], blocksT[0][:, 2:4], blocksT[1][:, 0:2]
            wo_f = blocksT[1][:, 2:4]
            wq_f, wk_f, wv_f = (w.rearrange("p a b c d -> p (a b c d)") for w in (wq_f, wk_f, wv_f))
            wo_f = wo_f.rearrange("p a b c d -> p (a b c d)").rearrange("p (h n) -> p h n", h=HP)
            wvT = [probsT[0][:, 2 * odd:2 * odd + 2].rearrange("p a b c d -> p (a b c d)")
                   .rearrange("p (h n) -> p h n", h=HP) for odd in range(2)]
            top = [sb(f"top{n}", [P, 2 * HP], to=ctx) for n in range(2)]
            total = [sb(f"total{n}", [P, 2 * HP], to=ctx) for n in range(2)]
            inverse = [sb(f"inverse{n}", [P, 2 * HP], to=ctx) for n in range(2)]

            score_bank, proj_bank, out_bank = bank[0:2], bank[2:6], bank[7]
            vo_bank = [bank[6], bank[7], bank[0], bank[1]]

            wq_loaded, wk_loaded = sem("wq_loaded", ctx), sem("wk_loaded", ctx)
            wv_loaded, wo_loaded = [sem(f"wv_loaded{n}", ctx) for n in range(2)], sem("wo_loaded", ctx)
            w12_loaded, w12_hi = sem("w12_loaded", ctx), sem("w12_hi", ctx)
            w12_ready = sem("w12_ready", ctx)
            biases_loaded = sem("biases_loaded", ctx)
            zeroed, ident_ready = sem("zeroed", ctx), sem("ident_ready", ctx)
            padded = sem("padded", ctx)
            w_turned = sem("w_turned", ctx)
            w_act, w_dve = sem("w_act", ctx), sem("w_dve", ctx)
            vo_ready = sem("vo_ready", ctx)
            weights_hi = sem("weights_hi", ctx)
            weights_lo = sem("weights_lo", ctx)
            arrived = [[sem(f"{of}_arrived{n}", ctx) for n in range(2)] for of in "xc"]
            x1_loaded = sem("x1_loaded", ctx)
            inputs_turned = sem("inputs_turned", ctx)
            hi_ready = sem("hi_ready", ctx)
            lo_ready = sem("lo_ready", ctx)
            bias_added = sem("bias_added", ctx)
            proj_ready = sem("proj_ready", ctx)
            proj_act = sem("proj_act", ctx)
            proj_dve = sem("proj_dve", ctx)
            scores_ready = sem("scores_ready", ctx)
            top_ready = sem("top_ready", ctx)
            shifted = sem("shifted", ctx)
            exp_ready = sem("exp_ready", ctx)
            total_ready = sem("total_ready", ctx)
            inverse_ready = sem("inverse_ready", ctx)
            probs_ready = sem("probs_ready", ctx)
            probs_turned = sem("probs_turned", ctx)
            moved = [sem(f"moved{n}", ctx) for n in range(2)]
            last_turned = sem("last_turned", ctx)
            probsT_act = sem("probsT_act", ctx)
            probsT_dve = sem("probsT_dve", ctx)
            out_ready = sem("out_ready", ctx)
            out_added = sem("out_added", ctx)

            with ExitStack() as place:
                kT = [sb(f"kT{n}", [P, HP, 2, 4, length], to=place) for n in range(2)]
                wqT = sb("wqT", [P, HP, dim], to=place)
                wkT = [sb(f"wkT{odd}", [P, HP, dim], to=place) for odd in range(2)]
            hidden = [sb(f"hidden{n}", [P, FC, FT], to=ctx) for n in range(2)]
            hidden_hi = [sb(f"hidden_hi{n}", [P, FC, FT], FP32R, ctx) for n in range(2)]
            hidden_lo = [sb(f"hidden_lo{n}", [P, FC, FT], FP32R, ctx) for n in range(2)]
            x1_in = [blocksT[0][:, n, :, :, :].rearrange("p q t h -> p (q t h)").rearrange(
                "p (t n) -> p t n", t=4) for n in range(2)]
            m_flat = [w[:, :, :, :].rearrange("p h s n -> p (h s n)") for w in (m_hi, m_lo)]
            x1T_hi, x1T_lo = ([w[:, n * FT:(n + 1) * FT] for n in range(2)] for w in m_flat)
            w1_hi, w1_lo = (w[:, 2 * FT:2 * FT + ff] for w in m_flat)
            w2_hi, w2_lo = (w[:, 2 * FT + ff:2 * FT + 2 * ff].rearrange("p (c n) -> p c n", c=FC) for w in m_flat)
            yT = [blocksT[1][:, n, :, :, :].rearrange("p q t h -> p (q t h)") for n in range(2)]
            y = [blocksT[1][:, 2 + n, :, :, :].rearrange("p q t h -> p (q t h)").rearrange(
                "p (t n) -> p t n", t=4) for n in range(2)]
            up_bank, down_bank, in_bank, back_bank = bank[0:4], proj_bank[2], bank[6], out_bank

            copied = sem("copied", ctx)
            x1_turned = sem("x1_turned", ctx)
            x1_hi_ready = sem("x1_hi_ready", ctx)
            x1_lo_ready = sem("x1_lo_ready", ctx)
            up_ready = sem("up_ready", ctx)
            hidden_ready = sem("hidden_ready", ctx)
            hidden_hi_ready = sem("hidden_hi_ready", ctx)
            hidden_lo_ready = sem("hidden_lo_ready", ctx)
            down_ready = sem("down_ready", ctx)
            yT_ready = sem("yT_ready", ctx)
            y_turned = sem("y_turned", ctx)
            y_ready = sem("y_ready", ctx)
            stored = [sem(f"stored{n}", ctx) for n in range(2)]

            def steps_without_keys(p):
                return 1 if isinstance(p, int) and p == PAIRS - 1 else 0

            def proj_made(p, n):
                if isinstance(p, int) and p < 0:
                    return 4 * p + 8 + n - 3
                return 8 * p + 8 + n + 1 - 4 * steps_without_keys(p)

            def taken(p, n):
                if n == 3:
                    return proj_dve, p + 1
                if isinstance(p, int) and p < 0:
                    return proj_act, 4 * p + 8 + n - 3
                return proj_act, 7 * p + 8 + (n + 1 if n < 3 else n) - 4 * steps_without_keys(p)

            with nc.Block() as block:

                @block.sync
                def _(sp):
                    def load_blocks(of, t, n):
                        for q in range(4):
                            sp.dma_start(blocks[of][n][q * Q:(q + 1) * Q, :, :, :],
                                         block_rows[of][q][:, bass.ds(t, 2), :, :]).then_inc(arrived[of][n], 16)

                    for n in range(2):
                        half = slice(n * inner // 2, (n + 1) * inner // 2)
                        sp.dma_start(wv_f[:, half], wv[:, half]).then_inc(wv_loaded[n], 16)
                    sp.dma_start(wk_f[:, :], wk).then_inc(wk_loaded, 16)
                    sp.dma_start(wq_f[:, :], wq).then_inc(wq_loaded, 16)
                    sp.dma_start(wo_f[:, :, :], wo.rearrange("(h p) n -> p h n", p=P)).then_inc(wo_loaded, 16)
                    load_blocks(1, 0, 0)
                    load_blocks(0, 0, 0)
                    load_blocks(0, 2, 1)
                    load_blocks(1, 2, 1)
                    sp.dma_start(bo_all[:, :], bo.partition_broadcast(P)).then_inc(biases_loaded, 16)
                    with nc.allow_non_contiguous_dma(reason="512 biases, once"):
                        sp.dma_start(b1_col[:, :], b1.rearrange("(c p) -> p c", p=P)).then_inc(biases_loaded, 16)
                        sp.dma_start(b2_col[:, :], b2.rearrange("(p o) -> p o", o=1)).then_inc(biases_loaded, 16)
                    sp.dma_start(w1_f[:, :], w1).then_inc(w12_loaded, 16)
                    sp.dma_start(w2_f[:, :, :], w2.rearrange("(c p) n -> p c n", p=P)).then_inc(w12_loaded, 16)

                    def load_x1(q):
                        ts = slice(q * PAIRS // 4, (q + 1) * PAIRS // 4)
                        sp.dma_start(x1[:, ts, :], x_rows[:, ts, :]).then_inc(x1_loaded, 16)

                    def load(i, n):
                        sp.wait_ge(inputs_turned, 4 * i + 2 * n - 2)
                        for of in range(2):
                            load_blocks(of, i * 4 + 2 * n, n)

                    def move(g, n):
                        sp.wait_ge(probs_turned, 4 * g + 4)
                        if not isinstance(g, int) or g > 1:
                            sp.wait_ge(out_ready, 2 * g - 2)
                        for a in range(4):
                            for b in range(4):
                                sp.dma_start(
                                    probsT[n][b * Q:(b + 1) * Q, a, :, :, :].rearrange("p q t h -> p (q t h)"),
                                    blocksT[n][a * Q:(a + 1) * Q, b, :, :, :].rearrange("p q t h -> p (q t h)")
                                ).then_inc(moved[n], 16)

                    load(1, 0)
                    load_x1(0)
                    load(1, 1)
                    for q in range(1, 4):
                        load_x1(q)
                    move(0, 0)
                    with sp.Fori(2, ROUNDS) as i:
                        load(i, 0)
                        move(2 * i - 3, 1)
                        load(i, 1)
                        move(2 * i - 2, 0)
                    move(GROUPS - 3, 1)
                    move(GROUPS - 2, 0)
                    with sp.Fori(0, FSTEPS // 2) as i:
                        for n in range(2):
                            sp.wait_ge(y_ready, 2 * i + n + 1)
                            sp.dma_start(out_rows[:, bass.ds(i * 8 + 4 * n, 4), :],
                                         y[n][:, :, :]).then_inc(stored[n], 16)
                    for n in range(2):
                        sp.wait_ge(stored[n], 16 * (FSTEPS // 2))

                @block.gpsimd
                def _(pool):
                    def add_bias(i, n):
                        at = x1[:, bass.ds(i * 4 + 2 * n, 2), :]
                        nc.gpsimd.tensor_tensor(at, at, bo_all[:, :].unsqueeze(1).broadcast_to([P, 2, dim]),
                                                ALU.add).then_inc(bias_added, 1)

                    def split_inputs(i, n):
                        pool.wait_ge(hi_ready, 2 * i + n + 1)
                        nc.gpsimd.tensor_tensor(cT_lo[n][:, :, 0:P], turned[1][n][:, :, :],
                                                cT_hi[n][:, :, 0:P].bitcast(FP32), ALU.subtract)
                        nc.gpsimd.tensor_tensor(cT_lo[n][:, :, P:P + length], turned[1][n][:, :, 0:length],
                                                cT_hi[n][:, :, 0:length].bitcast(FP32),
                                                ALU.subtract).then_inc(lo_ready, 1)

                    def normalise(i, j):
                        p = 4 * i + j
                        for h in range(2):
                            s = slice(h * HP, (h + 1) * HP)
                            v = probs[j % 2][:, s, :]
                            pool.wait_ge(exp_ready, 2 * p + h + 1)
                            pool.wait_ge(inverse_ready, 2 * p + h + 1)
                            nc.gpsimd.tensor_tensor(
                                v, v, inverse[j % 2][:, s].unsqueeze(2).broadcast_to([P, HP, length]),
                                ALU.mult).then_inc(probs_ready, 1)

                    def copy_x1(t, n):
                        pool.wait_ge(x1_turned, t - 1)
                        nc.gpsimd.tensor_copy(x1_in[n][:, :, :], x1[:, bass.ds(t * 4, 4), :]).then_inc(copied, 1)

                    nc.gpsimd.memset(ident[:, :], 0.0).then_inc(zeroed, 1)
                    pool.wait_ge(zeroed, 1)
                    nc.gpsimd.affine_select(out=ident[:, :], in_=ident[:, :], compare_op=ALU.not_equal,
                                            fill=1.0, base=0, pattern=[[-1, P]],
                                            channel_multiplier=1).then_inc(ident_ready, 1)
                    split_inputs(0, 0)
                    split_inputs(0, 1)
                    for j in range(4):
                        normalise(0, j)
                        if j % 2:
                            split_inputs(1, j // 2)
                        if j == 1:
                            pool.wait_ge(biases_loaded, 48)
                            pool.wait_ge(x1_loaded, 64)
                        if j % 2:
                            add_bias(0, j // 2)
                    add_bias(1, 0)
                    with pool.Fori(1, ROUNDS - 1) as i:
                        for j in range(4):
                            normalise(i, j)
                            if j % 2:
                                split_inputs(i + 1, j // 2)
                            if j % 2:
                                add_bias(i + j // 2, 1 - j // 2)
                    for j in range(2):
                        normalise(ROUNDS - 1, j)
                    add_bias(ROUNDS - 1, 1)
                    pool.wait_ge(proj_ready, proj_made(PAIRS - 3, 7))
                    pool.wait_ge(w12_loaded, 32)
                    nc.gpsimd.tensor_copy(w1_hi[:, :], w1_f[:, :]).then_inc(w12_hi, 1)
                    nc.gpsimd.tensor_copy(w2_hi[:, :, :], w2_f[:, :, :]).then_inc(w12_hi, 1)
                    pool.wait_ge(w12_hi, 1)
                    nc.gpsimd.tensor_tensor(w1_lo[:, :], w1_f[:, :], w1_hi[:, :].bitcast(FP32),
                                            ALU.subtract).then_inc(w12_ready, 1)
                    pool.wait_ge(w12_hi, 2)
                    nc.gpsimd.tensor_tensor(w2_lo[:, :, :], w2_f[:, :, :], w2_hi[:, :, :].bitcast(FP32),
                                            ALU.subtract).then_inc(w12_ready, 1)
                    for j in range(2, 4):
                        normalise(ROUNDS - 1, j)
                    pool.wait_ge(out_added, PAIRS)
                    with pool.Fori(0, (FSTEPS - 6) // 2) as i:
                        for n in range(2):
                            copy_x1(2 * i + n + 5, 1 - n)

                @block.tensor
                def _(pe):
                    def first_keys(which):
                        pe.wait_ge(lo_ready, 1)
                        for n in range(4):
                            if which:
                                pe.wait_ge(*taken(-2, 4 + n))
                            else:
                                pe.wait_ge(weights_lo, 5 + n)
                            make_keys(0, which, n)

                    def make_keys(n, which, bank_no):
                        h = HALF * which + bank_no
                        to = proj_bank[bank_no][:, :].rearrange("p (t s k) -> p t s k", t=2, k=length)
                        in_hi, in_lo = (w[n][:, :, 0:P].rearrange("p t (b k) -> p t b k", b=2)
                                        for w in (cT_hi, cT_lo))
                        for odd in range(2):
                            o = to[:, :, 1:3, :] if odd else to[:, :, 0:4:3, :]
                            nc.tensor.matmul(o, m_hi[:, h, odd, :], in_hi, start=True, stop=False)
                            nc.tensor.matmul(o, m_hi[:, h, odd, :], in_lo, start=False, stop=False)
                            last = nc.tensor.matmul(o, m_lo[:, h, odd, :], in_hi, start=False, stop=True)
                        last.then_inc(proj_ready, 1)

                    def scores(i, j):
                        p, g = 4 * i + j, j // 2
                        if j % 2 == 0:
                            pe.wait_ge(inputs_turned, 4 * i + 2 * g + 1)
                            pe.wait_ge(*taken(p - 1, 7))
                        for half in range(2):
                            if not isinstance(p, int) or p > 0:
                                pe.wait_ge(shifted, 2 * p - 1 + half)
                            for b in range(2):
                                last = nc.tensor.matmul(
                                    score_bank[half][b * length:(b + 1) * length, :],
                                    turned[0][g][:, j % 2, b * length:(b + 1) * length],
                                    kT[g][:, half * HALF:(half + 1) * HALF, j % 2, 2 * b:2 * b + 2, :]
                                    .rearrange("p h s k -> p h (s k)"),
                                    start=True, stop=True)
                            last.then_inc(scores_ready, 1)

                    def make_cvo(i, j):
                        p, g = 4 * i + j, j // 2
                        pe.wait_ge(lo_ready, 2 * i + g + 1)
                        for n in range(4):
                            odd, hs = n // 2, slice(4 * (n % 2), 4 * (n % 2) + 4)
                            pe.wait_ge(*taken(p - 1, n if steps_without_keys(p) else 4 + n))
                            rows = slice(odd * length, odd * length + P)
                            c_hi, c_lo = cT_hi[g][:, j % 2, rows], cT_lo[g][:, j % 2, rows]
                            w_hi = vo_hi[:, odd, hs, :].rearrange("p h n -> p (h n)")
                            w_lo = vo_lo[:, odd, hs, :].rearrange("p h n -> p (h n)")
                            nc.tensor.matmul(proj_bank[n][:, :], c_hi, w_hi, start=True, stop=False)
                            nc.tensor.matmul(proj_bank[n][:, :], c_hi, w_lo, start=False, stop=False)
                            nc.tensor.matmul(proj_bank[n][:, :], c_lo, w_hi, start=False,
                                             stop=True).then_inc(proj_ready, 1)

                    def attend(p, j):
                        if isinstance(p, int) and p >= PAIRS - 2:
                            pe.wait_ge(probsT_act, p - PAIRS + 3)
                            pe.wait_ge(probsT_dve, p - PAIRS + 3)
                        else:
                            pe.wait_ge(moved[j // 2], (p - j) * 64 + 256)
                        pe.wait_ge(*taken(p, 2))
                        pe.wait_ge(*taken(p, 3))
                        if not isinstance(p, int) or p > 0:
                            pe.wait_ge(out_added, p)
                        for h in range(HP):
                            for b in range(2):
                                last = nc.tensor.matmul(out_bank[b * length:(b + 1) * length, 0:dim],
                                                        probsT[j // 2][:, 2 * b:2 * b + 2, :, j % 2, h]
                                                        .rearrange("p a q -> p (a q)"),
                                                        cvo[j][:, b, h, :], start=h == 0, stop=h == HP - 1)
                        last.then_inc(out_ready, 1)

                    def turn_last(t, h):
                        pe.wait_ge(probs_ready, 2 * (PAIRS - 2 + t) + h + 1)
                        pe.wait_ge(*taken(PAIRS - 1, 2 * t + h))
                        for n in range(HALF):
                            at = 2 * (h * HALF + n)
                            last = nc.tensor.transpose(
                                proj_bank[2 * t + h][:, n * P:(n + 1) * P],
                                probs[t][:, at:at + 2, :].rearrange("p s k -> p (s k)"), ident[:, :])
                        last.then_inc(last_turned, 1)

                    def step(i, j, more):
                        p, g = 4 * i + j, j // 2
                        if not isinstance(p, int) or p >= 4:
                            attend(p - 4, j)
                        make_cvo(i, j)
                        scores(i, j)
                        if more or j < 2:
                            for n in range(4):
                                key_bank(i, j, n)

                    def key_bank(i, j, n):
                        p, g = 4 * i + j, j // 2
                        pe.wait_ge(lo_ready, 2 * i + g + 2)
                        pe.wait_ge(*taken(p, n))
                        make_keys((g + 1) % 2, j % 2, n)

                    def turn_x1(t, n, before):
                        if isinstance(t, int):
                            pe.wait_ge(out_added, 4 * t + 4)
                        else:
                            pe.wait_ge(copied, t - 4)
                        if before:
                            pe.wait_ge(x1_lo_ready, t)
                        for s in range(4):
                            src = x1[:, 4 * t + s, :] if isinstance(t, int) else x1_in[n][:, s, :]
                            last = nc.tensor.transpose(in_bank[:, s * P:(s + 1) * P], src, ident[:, :])
                        last.then_inc(x1_turned, 1)

                    def up(t, n, before, chunks=range(FC)):
                        if isinstance(t, int) and t == 0:
                            pe.wait_ge(w12_ready, 2)
                        pe.wait_ge(x1_hi_ready, t + 1)
                        pe.wait_ge(x1_lo_ready, t + 1)
                        for c in chunks:
                            if before:
                                pe.wait_ge(hidden_ready, FC * t - FC + c + 1)
                            cols = slice(c * P, (c + 1) * P)
                            nc.tensor.matmul(up_bank[c][:, :], w1_hi[:, cols], x1T_hi[n][:, :], start=True, stop=False)
                            nc.tensor.matmul(up_bank[c][:, :], w1_hi[:, cols], x1T_lo[n][:, :], start=False, stop=False)
                            nc.tensor.matmul(up_bank[c][:, :], w1_lo[:, cols], x1T_hi[n][:, :], start=False,
                                             stop=True).then_inc(up_ready, 1)

                    def down(t, n, before):
                        if before:
                            pe.wait_ge(yT_ready, t)
                        else:
                            pe.wait_ge(probsT_act, 2)
                        for c in range(FC):
                            pe.wait_ge(hidden_hi_ready, FC * t + c + 1)
                            nc.tensor.matmul(down_bank[:, :], w2_hi[:, c, :], hidden_hi[n][:, c, :], start=c == 0, stop=False)
                            nc.tensor.matmul(down_bank[:, :], w2_lo[:, c, :], hidden_hi[n][:, c, :], start=False, stop=False)
                            pe.wait_ge(hidden_lo_ready, FC * t + c + 1)
                            last = nc.tensor.matmul(down_bank[:, :], w2_hi[:, c, :], hidden_lo[n][:, c, :],
                                                    start=False, stop=c == FC - 1)
                        last.then_inc(down_ready, 1)

                    def turn_y(t, n, before):
                        pe.wait_ge(yT_ready, t + 1)
                        if before:
                            pe.wait_ge(y_ready, t)
                        else:
                            pe.wait_ge(out_added, PAIRS)
                        for s in range(4):
                            last = nc.tensor.transpose(back_bank[:, s * P:(s + 1) * P], yT[n][:, s * P:(s + 1) * P],
                                                       ident[:, :])
                        last.then_inc(y_turned, 1)

                    pe.wait_ge(ident_ready, 1)
                    for w, (src, at) in enumerate(((wv_f, 0), (wk_f, 2), (wq_f, 4))):
                        for h in range(HP):
                            if w == 0 and h % 4 == 0:
                                pe.wait_ge(wv_loaded[h // 4], 16)
                            if w and h == 0:
                                pe.wait_ge((wk_loaded, wq_loaded)[w - 1], 16)
                            last = nc.tensor.transpose(bank[at + h // 4][:, (h % 4) * P:(h % 4 + 1) * P],
                                                       src[:, h * P:(h + 1) * P], ident[:, :])
                            if h % 4 == 3:
                                last.then_inc(w_turned, 1)
                    pe.wait_ge(padded, 4)
                    pe.wait_ge(wo_loaded, 16)
                    pe.wait_ge(w_act, 1)
                    pe.wait_ge(w_dve, 1)
                    for odd in range(2):
                        for h in range(HP):
                            last = nc.tensor.matmul(vo_bank[2 * odd + h // 4][:, (h % 4) * P:(h % 4 + 1) * P],
                                                    wvT[odd][:, h, :], wo_f[:, h, :], start=True, stop=True)
                            if h % 4 == 3:
                                last.then_inc(vo_ready, 1)
                    pe.wait_ge(w_act, 3)
                    pe.wait_ge(w_dve, 3)
                    for h in range(HP):
                        for odd in range(2):
                            at = (2 * h + odd) % 4
                            last = nc.tensor.matmul(proj_bank[h // 2][:, at * P:(at + 1) * P],
                                                    wkT[odd][:, h, :], wqT[:, h, :], start=True, stop=True)
                        if h % 2:
                            last.then_inc(vo_ready, 1)
                    first_keys(0)
                    first_keys(1)
                    for j in range(4):
                        step(0, j, True)
                    with pe.Fori(1, ROUNDS - 1) as i:
                        for j in range(4):
                            step(i, j, True)
                    for j in range(4):
                        if j == 3:
                            turn_x1(0, 0, False)
                        step(ROUNDS - 1, j, False)
                    turn_last(0, 0)
                    turn_last(0, 1)
                    pe.wait_ge(shifted, 2 * PAIRS - 1)
                    up(0, 0, False, [0])
                    attend(PAIRS - 4, 0)
                    pe.wait_ge(shifted, 2 * PAIRS)
                    up(0, 0, False, [1])
                    pe.wait_ge(probsT_act, 1)
                    pe.wait_ge(probsT_dve, 1)
                    up(0, 0, False, range(2, FC))
                    turn_x1(1, 1, True)
                    turn_last(1, 0)
                    turn_last(1, 1)
                    attend(PAIRS - 3, 1)
                    up(1, 1, True, range(2))
                    attend(PAIRS - 2, 2)
                    up(1, 1, True, range(2, FC))
                    attend(PAIRS - 1, 3)
                    turn_x1(2, 0, True)
                    down(0, 0, False)
                    up(2, 0, True)
                    turn_x1(3, 1, True)
                    down(1, 1, True)
                    turn_y(0, 0, False)
                    up(3, 1, True)
                    turn_x1(4, 0, True)
                    down(2, 0, True)
                    turn_y(1, 1, True)
                    with pe.Fori(2, FSTEPS // 2 - 1) as i:
                        for n in range(2):
                            up(2 * i + n, n, True)
                            turn_x1(2 * i + n + 1, 1 - n, True)
                            down(2 * i + n - 1, 1 - n, True)
                            turn_y(2 * i + n - 2, n, True)
                    t = FSTEPS - 2
                    up(t, 0, True)
                    turn_x1(t + 1, 1, True)
                    down(t - 1, 1, True)
                    turn_y(t - 2, 0, True)
                    up(t + 1, 1, True)
                    down(t, 0, True)
                    turn_y(t - 1, 1, True)
                    down(t + 1, 1, True)
                    turn_y(t, 0, True)
                    turn_y(t + 1, 1, True)

                @block.scalar
                def _(act):
                    def round_inputs(i, n):
                        act.wait_ge(inputs_turned, 4 * i + 2 * n + 2)
                        nc.scalar.activation(cT_hi[n][:, :, 0:P], turned[1][n][:, :, :], ACT.Copy)
                        nc.scalar.activation(cT_hi[n][:, :, P:P + length], turned[1][n][:, :, 0:length],
                                             ACT.Copy).then_inc(hi_ready, 1)

                    def take_keys(n, which, bank_no, made):
                        act.wait_ge(proj_ready, made)
                        nc.scalar.activation(kT[n][:, HALF * which + bank_no, :, :, :].rearrange("p t s k -> p (t s k)"),
                                             proj_bank[bank_no][:, :], ACT.Copy).then_inc(proj_act, 1)

                    def exponentials(i, j, h):
                        p = 4 * i + j
                        v = probs[j % 2][:, h * HP:(h + 1) * HP, :]
                        act.wait_ge(shifted, 2 * p + h + 1)
                        nc.scalar.activation(v, v, ACT.Exp, scale=SCALE).then_inc(exp_ready, 1)

                    def take_cvo(i, j, n):
                        p = 4 * i + j
                        act.wait_ge(proj_ready, proj_made(p, n))
                        src = proj_bank[n][:, :].rearrange("p (h n) -> p h n", h=4)
                        odd, hs = n // 2, slice(4 * (n % 2), 4 * (n % 2) + 4)
                        nc.scalar.activation(cvo[j][0:length, odd, hs, :], src[0:length], ACT.Copy)
                        nc.scalar.activation(cvo[j][length:P, 1 - odd, hs, :], src[length:P],
                                             ACT.Copy).then_inc(proj_act, 1)

                    def take_last(t):
                        act.wait_ge(last_turned, 2 * t + 1)
                        nc.scalar.activation(probsT[1][:, :, :, t, 0:HALF].rearrange("p a q h -> p h a q"),
                                             proj_bank[2 * t][:, :].rearrange("p (h a q) -> p h a q", h=HALF, q=Q),
                                             ACT.Copy).then_inc(probsT_act, 1)

                    def step(i, j, more):
                        p, g = 4 * i + j, j // 2
                        for n in range(3):
                            take_cvo(i, j, n)
                        for n in (4, 5, 0, 6, 1, 7):
                            if n < 2:
                                exponentials(i, j, n)
                            elif more or j < 2:
                                take_keys((g + 1) % 2, j % 2, n - 4, proj_made(p, n))
                        if more and j % 2:
                            round_inputs(i + 1, g)

                    def round_x1(t, n):
                        act.wait_ge(x1_turned, t + 1)
                        nc.scalar.activation(x1T_hi[n][:, :], in_bank[:, :], ACT.Copy).then_inc(x1_hi_ready, 1)

                    def gelu(t, n):
                        for c in range(FC):
                            act.wait_ge(up_ready, FC * t + c + 1)
                            nc.scalar.activation(hidden[n][:, c, :], up_bank[c][:, :], ACT.Gelu,
                                                 bias=b1_col[:, c:c + 1]).then_inc(hidden_ready, 1)

                    def add_b2(t, n):
                        act.wait_ge(down_ready, t + 1)
                        nc.scalar.activation(yT[n][:, :], down_bank[:, :], ACT.Identity,
                                             bias=b2_col[:, 0:1]).then_inc(yT_ready, 1)

                    def forward(t, n, before):
                        if before:
                            act.wait_ge(hidden_lo_ready, FC * t - FC)
                        gelu(t, n)
                        round_x1(t + 1, 1 - n)
                        if before:
                            add_b2(t - 1, 1 - n)

                    def round_vo(n):
                        act.wait_ge(vo_ready, n + 1)
                        nc.scalar.activation(vo_hi[:, n // 2, 4 * (n % 2):4 * (n % 2) + 4, :],
                                             vo_bank[n][:, :].rearrange("p (h n) -> p h n", h=4),
                                             ACT.Copy).then_inc(weights_hi, 1)

                    for w, (src, to) in enumerate(((bank[0], wvT), (bank[2], wkT))):
                        src = src[:, :].rearrange("p (h n) -> p h n", h=4)
                        act.wait_ge(w_turned, 2 * w + 1)
                        nc.scalar.activation(to[0][0:d_head, 0:4, :], src[0:d_head], ACT.Copy)
                        nc.scalar.activation(to[1][d_head:P, 0:4, :], src[d_head:P], ACT.Copy).then_inc(w_act, 1)
                    act.wait_ge(w_turned, 5)
                    nc.scalar.activation(wqT[:, 0:4, :], bank[4][:, :].rearrange("p (h n) -> p h n", h=4),
                                         ACT.Copy).then_inc(w_act, 1)
                    round_inputs(0, 0)
                    for n in range(4):
                        round_vo(n)
                    for n in range(4):
                        act.wait_ge(vo_ready, n + 5)
                        nc.scalar.activation(m_hi[:, 2 * n:2 * n + 2, :, :].rearrange("p h s n -> p (h s n)"),
                                             proj_bank[n][:, :], ACT.Copy).then_inc(weights_hi, 1)
                    for which in range(2):
                        for n in range(4):
                            take_keys(0, which, n, proj_made(which - 2, 4 + n))
                    round_inputs(0, 1)
                    for j in range(4):
                        step(0, j, True)
                    with act.Fori(1, ROUNDS - 1) as i:
                        for j in range(4):
                            step(i, j, True)
                    for j in range(4):
                        if j == 3:
                            round_x1(0, 0)
                        step(ROUNDS - 1, j, False)
                    take_last(0)
                    gelu(0, 0)
                    round_x1(1, 1)
                    take_last(1)
                    gelu(1, 1)
                    round_x1(2, 0)
                    add_b2(0, 0)
                    with act.Fori(1, FSTEPS // 2 - 1) as i:
                        for n in range(2):
                            forward(2 * i + n, n, True)
                    t = FSTEPS - 2
                    forward(t, 0, True)
                    act.wait_ge(hidden_lo_ready, FC * t)
                    gelu(t + 1, 1)
                    add_b2(t, 0)
                    add_b2(t + 1, 1)

                @block.vector
                def _(dve):
                    def turn_inputs(i, n):
                        if not isinstance(i, int) or i > 0:
                            dve.wait_ge(lo_ready, 2 * i + n - 1)
                        for of in range(2):
                            dve.wait_ge(arrived[of][n], 64 * i + 64)
                            nc.vector.transpose(turned[of][n][:, :, :].rearrange("p t n -> p (t n)"),
                                                blocks[of][n][:, :, :, :].rearrange("p t a n -> p (t a n)")
                                                ).then_inc(inputs_turned, 1)

                    def shift(i, j, h):
                        p = 4 * i + j
                        s = slice(h * HP, (h + 1) * HP)
                        v = score_bank[h][:, :].rearrange("p (s k) -> p s k", k=length)
                        dve.wait_ge(scores_ready, 2 * p + h + 1)
                        nc.vector.reduce_max(top[j % 2][:, s], v, AX.X).then_inc(top_ready, 1)
                        if not isinstance(p, int) or p > 1:
                            dve.wait_ge(probs_turned, 2 * p + h - 3)
                        dve.wait_ge(top_ready, 2 * p + h + 1)
                        nc.vector.tensor_tensor(probs[j % 2][:, s, :], v,
                                                top[j % 2][:, s].unsqueeze(2).broadcast_to([P, HP, length]),
                                                ALU.subtract).then_inc(shifted, 1)

                    def take_cvo(i, j):
                        p = 4 * i + j
                        dve.wait_ge(proj_ready, proj_made(p, 3))
                        src = proj_bank[3][:, :].rearrange("p (h n) -> p h n", h=4)
                        nc.vector.tensor_copy(cvo[j][0:length, 1, HALF:HP, :], src[0:length])
                        nc.vector.tensor_copy(cvo[j][length:P, 0, HALF:HP, :],
                                              src[length:P]).then_inc(proj_dve, 1)

                    def turn_blocks(p, j):
                        g = j // 2
                        if not isinstance(p, int) or p >= 4:
                            dve.wait_ge(moved[g], (p - j) * 64)
                        for h in range(2):
                            hs = slice(h * HALF, (h + 1) * HALF)
                            dve.wait_ge(probs_ready, 2 * p + h + 1)
                            nc.vector.transpose(
                                blocksT[g][:, :, :, j % 2, hs].rearrange("p b q h -> p h b q"),
                                probs[j % 2][:, h * HP:(h + 1) * HP, :].rearrange(
                                    "p (h s) (c k) -> p h (s c) k", s=2, k=Q)).then_inc(probs_turned, 1)

                    def invert_sums(p, n, h):
                        s = slice(h * HP, (h + 1) * HP)
                        dve.wait_ge(exp_ready, 2 * p + h + 1)
                        nc.vector.reduce_sum(total[n][:, s], probs[n][:, s, :], AX.X).then_inc(total_ready, 1)
                        dve.wait_ge(total_ready, 2 * p + h + 1)
                        nc.vector.reciprocal(inverse[n][:, s], total[n][:, s]).then_inc(inverse_ready, 1)

                    def take_last(t):
                        dve.wait_ge(last_turned, 2 * t + 2)
                        nc.vector.tensor_copy(probsT[1][:, :, :, t, HALF:HP].rearrange("p a q h -> p h a q"),
                                              proj_bank[2 * t + 1][:, :].rearrange("p (h a q) -> p h a q", h=HALF, q=Q)
                                              ).then_inc(probsT_dve, 1)

                    def add_output(p, groups):
                        dve.wait_ge(bias_added, groups)
                        dve.wait_ge(out_ready, p + 1)
                        at = x1[:, bass.ds(p, 1), :].rearrange("p o n -> p (o n)")
                        nc.vector.tensor_tensor(at, out_bank[:, 0:dim], at, ALU.add).then_inc(out_added, 1)

                    def step(i, j, more):
                        p, g = 4 * i + j, j // 2
                        static = isinstance(p, int)
                        if not static or p > 0:
                            invert_sums(p - 1, (j + 1) % 2, 0)
                            invert_sums(p - 1, (j + 1) % 2, 1)
                        if not static or p >= 4:
                            add_output(p - 4, 2 * i + g - 1)
                        if static and p == PAIRS - 1:
                            split_x1(0, 0)
                        if not static or 0 < p < PAIRS - 1:
                            turn_blocks(p - 1, (j + 3) % 4)
                        take_cvo(i, j)
                        shift(i, j, 0)
                        shift(i, j, 1)
                        if more and j % 2:
                            turn_inputs(i + 1, g)

                    def split_x1(t, n):
                        dve.wait_ge(x1_hi_ready, t + 1)
                        nc.vector.tensor_tensor(x1T_lo[n][:, :], in_bank[:, :], x1T_hi[n][:, :].bitcast(FP32),
                                                ALU.subtract).then_inc(x1_lo_ready, 1)

                    def split_hidden(t, n, chunks):
                        for c in chunks:
                            dve.wait_ge(hidden_ready, FC * t + c + 1)
                            nc.vector.tensor_copy(hidden_hi[n][:, c, :], hidden[n][:, c, :]).then_inc(hidden_hi_ready, 1)
                            dve.wait_ge(hidden_hi_ready, FC * t + c + 1)
                            nc.vector.tensor_tensor(hidden_lo[n][:, c, :], hidden[n][:, c, :],
                                                    hidden_hi[n][:, c, :].bitcast(FP32),
                                                    ALU.subtract).then_inc(hidden_lo_ready, 1)

                    def add_x1(t, n, writes):
                        dve.wait_ge(y_turned, t + 1)
                        if writes is not None:
                            dve.wait_ge(stored[n], writes)
                        nc.vector.tensor_tensor(y[n][:, :, :], back_bank[:, :].rearrange("p (t n) -> p t n", t=4),
                                                x1[:, bass.ds(t * 4, 4), :], ALU.add).then_inc(y_ready, 1)

                    def forward(t, n, last):
                        split_hidden(t, n, range(FC - 1))
                        if not last:
                            split_x1(t + 1, 1 - n)
                        split_hidden(t, n, range(FC - 1, FC))

                    def split_vo(n):
                        hs = slice(4 * (n % 2), 4 * (n % 2) + 4)
                        nc.vector.tensor_tensor(
                            vo_lo[:, n // 2, hs, :], vo_bank[n][:, :].rearrange("p (h n) -> p h n", h=4),
                            vo_hi[:, n // 2, hs, :].bitcast(FP32), ALU.subtract).then_inc(weights_lo, 1)

                    for w in (wvT, wkT):
                        nc.vector.memset(w[0][d_head:P, :, :], 0.0).then_inc(padded, 1)
                        nc.vector.memset(w[1][0:d_head, :, :], 0.0).then_inc(padded, 1)
                    for w, (src, to) in enumerate(((bank[1], wvT), (bank[3], wkT))):
                        src = src[:, :].rearrange("p (h n) -> p h n", h=4)
                        dve.wait_ge(w_turned, 2 * w + 2)
                        nc.vector.tensor_copy(to[0][0:d_head, 4:8, :], src[0:d_head])
                        nc.vector.tensor_copy(to[1][d_head:P, 4:8, :], src[d_head:P]).then_inc(w_dve, 1)
                    dve.wait_ge(w_turned, 6)
                    nc.vector.tensor_copy(wqT[:, 4:8, :], bank[5][:, :].rearrange("p (h n) -> p h n", h=4)).then_inc(w_dve, 1)
                    turn_inputs(0, 0)
                    for n in range(4):
                        hs = slice(4 * (n % 2), 4 * (n % 2) + 4)
                        dve.wait_ge(weights_hi, 1 + n)
                        nc.vector.tensor_tensor(
                            vo_lo[:, n // 2, hs, :], vo_bank[n][:, :].rearrange("p (h n) -> p h n", h=4),
                            vo_hi[:, n // 2, hs, :].bitcast(FP32), ALU.subtract).then_inc(weights_lo, 1)
                    for n in range(4):
                        hs = slice(2 * n, 2 * n + 2)
                        dve.wait_ge(weights_hi, 5 + n)
                        nc.vector.tensor_tensor(
                            m_lo[:, hs, :, :].rearrange("p h s n -> p (h s n)"), proj_bank[n][:, :],
                            m_hi[:, hs, :, :].rearrange("p h s n -> p (h s n)").bitcast(FP32),
                            ALU.subtract).then_inc(weights_lo, 1)
                    turn_inputs(0, 1)
                    for j in range(4):
                        step(0, j, True)
                    with dve.Fori(1, ROUNDS - 1) as i:
                        for j in range(4):
                            step(i, j, True)
                    for j in range(4):
                        step(ROUNDS - 1, j, False)
                    for h in range(2):
                        invert_sums(PAIRS - 1, 1, h)
                    take_last(0)
                    split_hidden(0, 0, range(2))
                    add_output(PAIRS - 4, GROUPS)
                    split_x1(1, 1)
                    split_hidden(0, 0, range(2, FC))
                    take_last(1)
                    add_output(PAIRS - 3, GROUPS)
                    split_hidden(1, 1, range(1))
                    add_output(PAIRS - 2, GROUPS)
                    split_hidden(1, 1, range(1, 3))
                    add_output(PAIRS - 1, GROUPS)
                    split_x1(2, 0)
                    split_hidden(1, 1, range(3, FC))
                    for t in range(2, 4):
                        forward(t, t % 2, False)
                        add_x1(t - 2, t % 2, None)
                    with dve.Fori(2, FSTEPS // 2 - 1) as i:
                        for n in range(2):
                            forward(2 * i + n, n, False)
                            add_x1(2 * i + n - 2, n, 16 * i - 16)
                    for t in range(FSTEPS - 2, FSTEPS):
                        forward(t, t % 2, t == FSTEPS - 1)
                        add_x1(t - 2, t % 2, 16 * (t // 2) - 16)
                    for t in range(FSTEPS, FSTEPS + 2):
                        add_x1(t - 2, t % 2, 16 * (t // 2) - 16)


_INS = ["x", "ctx_1024", "L0_xattn_Wq", "L0_xattn_Wk", "L0_xattn_Wv", "L0_xattn_Wo", "L0_xattn_bo",
        "L0_xattn_W1", "L0_xattn_b1", "L0_xattn_W2", "L0_xattn_b2"]


def kernel(**inputs):
    import numpy as _np
    import concourse.bacc as _bacc
    from concourse import mybir as _mybir
    from concourse.bass_utils import run_bass_kernel_spmd as _run

    nc = _bacc.Bacc("TRN2", target_bir_lowering=False, num_devices=1)
    arrays, args = {}, []
    for name in _INS:
        a = _np.ascontiguousarray(inputs[name])
        arrays[f"in_{name}_dram"] = a
        args.append(nc.dram_tensor(f"in_{name}_dram", a.shape, _mybir.dt.from_np(a.dtype), kind="ExternalInput").ap())
    out = nc.dram_tensor("out_dram", inputs["x"].shape, _mybir.dt.float32, kind="ExternalOutput").ap()
    cross_attention_block(nc, *args, out)
    return _run(nc, [arrays], core_ids=[0]).results[0]["out_dram"]
```
